# Optimizing a Trainium2 kernel written in Bass

```python
import numpy as np
import jax
import jax.numpy as jnp

def _softmax(x, axis=-1):
    return jax.nn.softmax(x, axis=axis)

def _gelu(x):
    return jax.nn.gelu(x, approximate=True)

def _silu(x):
    return jax.nn.silu(x)

def _sigmoid(x):
    return jax.nn.sigmoid(x)

def _layernorm(x, axis=-1, eps=1e-05):
    m = jnp.mean(x, axis=axis, keepdims=True)
    v = jnp.var(x, axis=axis, keepdims=True)
    return (x - m) / jnp.sqrt(v + eps)

def _scatter_add(tgt, idx, src, axis=0):
    return tgt.at[idx].add(src)

def _segment_sum(src, seg, n):
    return jax.ops.segment_sum(src, seg, n)
kernel_name = 'mk_decoder_postln_d1_seqx_r8_333bfc'

def setup_inputs(seed: int=0):
    np.random.seed(seed)
    _w = jnp.asarray

    def _rec_inputs():
        import jax
        import jax.numpy as jnp
        _rk = jax.random.key(seed)
        x = 7.22e-05 + 1 * jax.random.normal(jax.random.fold_in(_rk, 1), (8, 128, 128), jnp.float32)
        _lenS = 128 - jax.random.randint(jax.random.fold_in(_rk, 7), (8,), 0, max(1, 128 // 4) + 1, jnp.int32)
        _lenS2 = 128 - jax.random.randint(jax.random.fold_in(_rk, 8), (8,), 0, max(1, 128 // 4) + 1, jnp.int32)
        _ctx_1024P = jax.random.normal(jax.random.fold_in(_rk, 11), (8, 16, 128), jnp.float32)
        _ctx_1024c = jax.random.dirichlet(jax.random.fold_in(_rk, 511), 0.3 * jnp.ones((16,), jnp.float32), (8, 128))
        _ctx_1024t = jnp.einsum('bsk,bkd->bsd', _ctx_1024c, _ctx_1024P)
        _ctx_1024t = _ctx_1024t * jax.lax.rsqrt(jnp.mean(jnp.square(_ctx_1024t)) + 1e-12) * 0.953939
        ctx_1024 = 4.13588e-05 + 0.999923 * (_ctx_1024t + 0.3 * jax.random.normal(jax.random.fold_in(_rk, 611), (8, 128, 128), jnp.float32))
        _validS = jnp.arange(128)[None, :] < _lenS[:, None]
        _validS2 = jnp.arange(128)[None, :] < _lenS2[:, None]
        _causal = jnp.tril(jnp.ones((128, 128), dtype=bool))
        mask_BxSxS2_ik1 = jnp.where(jnp.broadcast_to(_validS2[:, None, :], (8, 128, 128)), 1, 0).astype(jnp.int32)
        return (x, ctx_1024, mask_BxSxS2_ik1)
    x, ctx_1024, mask_BxSxS2_ik1 = _rec_inputs()

    def _L0_attn_setup():
        import jax, jax.numpy as jnp
        import numpy as np
        B, S, D = (2, 256, 128)
        H, DQ, DV = (16, 64, 64)
        key = jax.random.key(seed)
        k1, k2, k3, k4, k5 = jax.random.split(key, 5)
        scale = 0.02
        return {'x': jax.random.normal(k1, (B, S, D), dtype=jnp.float32), 'w_q': jax.random.normal(k2, (H, DQ, D), dtype=jnp.float32) * scale, 'w_k': jax.random.normal(k3, (H, DQ, D), dtype=jnp.float32) * scale, 'w_v': jax.random.normal(k4, (H, DV, D), dtype=jnp.float32) * scale, 'w_o': jax.random.normal(k5, (D, H * DV), dtype=jnp.float32) * scale}
    _L0_attn_all = _L0_attn_setup()
    _L0_attn_in = {k: v for k, v in _L0_attn_all.items() if k in ('w_q', 'w_k', 'w_v', 'w_o')}
    del _L0_attn_all

    def _L0_xattn_setup():
        import jax, jax.numpy as jnp
        import numpy as np
        H = 16
        D_MODEL = 128
        DK = D_MODEL // H
        NEG = -1000000000.0

        def _split_heads(x, B, S):
            return x.reshape(B, S, H, DK).transpose(0, 2, 1, 3)
        key = jax.random.key(seed)
        ks = jax.random.split(key, 13)
        B, S, D = (4, 256, D_MODEL)
        scale = 1.0 / np.sqrt(D)
        inp = {'q': jax.random.normal(ks[0], (B, S, D), jnp.float32), 'k': jax.random.normal(ks[1], (B, S, D), jnp.float32), 'v': jax.random.normal(ks[2], (B, S, D), jnp.float32), 'mask': jax.random.randint(ks[3], (B, S, S), 0, 2, jnp.int32), 'Wq': jax.random.normal(ks[4], (D, D), jnp.float32) * scale, 'bq': jnp.zeros((D,), jnp.float32), 'Wk': jax.random.normal(ks[5], (D, D), jnp.float32) * scale, 'bk': jnp.zeros((D,), jnp.float32), 'Wv': jax.random.normal(ks[6], (D, D), jnp.float32) * scale, 'bv': jnp.zeros((D,), jnp.float32), 'Wo': jax.random.normal(ks[7], (D, D), jnp.float32) * scale, 'bo': jnp.zeros((D,), jnp.float32)}
        return inp
    _L0_xattn_all = _L0_xattn_setup()
    _L0_xattn_in = {k: v for k, v in _L0_xattn_all.items() if k in ('Wq', 'bq', 'Wk', 'bk', 'Wv', 'bv', 'Wo', 'bo')}
    del _L0_xattn_all

    def _L0_ffn_setup():
        import jax, jax.numpy as jnp
        import numpy as np
        JITTER_EPS = 0.01
        NEG_INF = -jnp.inf

        def sparsemixer_eval(scores, jitter_eps):
            m1 = jnp.max(scores, axis=-1, keepdims=True)
            ind1 = jnp.argmax(scores, axis=-1)
            factor1 = jnp.maximum(jnp.abs(scores), m1)
            mask1 = jax.lax.stop_gradient((m1 - scores) / factor1 > 2.0 * jitter_eps)
            gates1 = jax.nn.softmax(jnp.where(mask1, NEG_INF, scores), axis=-1)
            mult1 = jnp.take_along_axis(gates1, ind1[:, None], axis=-1)[:, 0]
            E = scores.shape[-1]
            onehot1 = ind1[:, None] == jnp.arange(E)[None, :]
            masked_scores = jnp.where(onehot1, NEG_INF, scores)
            m2 = jnp.max(masked_scores, axis=-1, keepdims=True)
            ind2 = jnp.argmax(masked_scores, axis=-1)
            factor2 = jnp.maximum(jnp.abs(scores), m2)
            mask2 = jax.lax.stop_gradient((m2 - scores) / factor2 > 2.0 * jitter_eps)
            gates2 = jax.nn.softmax(jnp.where(mask2, NEG_INF, masked_scores), axis=-1)
            mult2 = jnp.take_along_axis(gates2, ind2[:, None], axis=-1)[:, 0]
            multiplier = jnp.stack([mult1, mult2], axis=-1)
            selected = jnp.stack([ind1, ind2], axis=-1)
            return (multiplier, selected)
        key = jax.random.key(seed)
        k0, k1, k2, k3, k4 = jax.random.split(key, 5)
        B, S, H, F, E = (2, 128, 128, 256, 8)
        scale = 0.02
        return {'hidden_states': jax.random.normal(k0, (B, S, H), dtype=jnp.float32), 'router_w': jax.random.normal(k1, (E, H), dtype=jnp.float32) * scale, 'w_gate': jax.random.normal(k2, (E, F, H), dtype=jnp.float32) * scale, 'w_up': jax.random.normal(k3, (E, F, H), dtype=jnp.float32) * scale, 'w_down': jax.random.normal(k4, (E, H, F), dtype=jnp.float32) * scale}
    _L0_ffn_all = _L0_ffn_setup()
    _L0_ffn_in = {k: v for k, v in _L0_ffn_all.items() if k in ('router_w', 'w_gate', 'w_up', 'w_down')}
    del _L0_ffn_all
    return {'x': x, 'ctx_1024': ctx_1024, 'mask_BxSxS2_ik1': mask_BxSxS2_ik1, 'L0_attn_w_q': _L0_attn_in['w_q'], 'L0_attn_w_k': _L0_attn_in['w_k'], 'L0_attn_w_v': _L0_attn_in['w_v'], 'L0_attn_w_o': _L0_attn_in['w_o'], 'L0_xattn_Wq': _L0_xattn_in['Wq'], 'L0_xattn_bq': _L0_xattn_in['bq'], 'L0_xattn_Wk': _L0_xattn_in['Wk'], 'L0_xattn_bk': _L0_xattn_in['bk'], 'L0_xattn_Wv': _L0_xattn_in['Wv'], 'L0_xattn_bv': _L0_xattn_in['bv'], 'L0_xattn_Wo': _L0_xattn_in['Wo'], 'L0_xattn_bo': _L0_xattn_in['bo'], 'L0_ffn_router_w': _L0_ffn_in['router_w'], 'L0_ffn_w_gate': _L0_ffn_in['w_gate'], 'L0_ffn_w_up': _L0_ffn_in['w_up'], 'L0_ffn_w_down': _L0_ffn_in['w_down']}

def reference(x, ctx_1024, mask_BxSxS2_ik1, L0_attn_w_q, L0_attn_w_k, L0_attn_w_v, L0_attn_w_o, L0_xattn_Wq, L0_xattn_bq, L0_xattn_Wk, L0_xattn_bk, L0_xattn_Wv, L0_xattn_bv, L0_xattn_Wo, L0_xattn_bo, L0_ffn_router_w, L0_ffn_w_gate, L0_ffn_w_up, L0_ffn_w_down):
    import jax
    import jax.numpy as jnp

    def _L0_attn_ref(x, w_q, w_k, w_v, w_o):
        import jax, jax.numpy as jnp
        import numpy as np
        B, S, D = (2, 256, 128)
        H, DQ, DV = (16, 64, 64)
        b, s, d = x.shape
        q = jnp.einsum('bsd,hqd->bhsq', x, w_q)
        k = jnp.einsum('bsd,hqd->bhsq', x, w_k)
        v = jnp.einsum('bsd,hvd->bhsv', x, w_v)
        scores = jnp.einsum('bhsq,bhtq->bhst', q, k)
        causal = jnp.triu(jnp.ones((s, s), dtype=bool), k=1)
        masked = jnp.where(causal, -jnp.inf, scores)
        dq = w_q.shape[1]
        weights = jax.nn.softmax(masked / jnp.sqrt(jnp.float32(dq)), axis=-1)
        out = jnp.einsum('bhst,bhtv->bhsv', weights, v)
        cat = out.transpose(0, 2, 1, 3).reshape(b, s, -1)
        return jnp.einsum('bsf,df->bsd', cat, w_o)

    def _L0_xattn_ref(q, k, v, mask, Wq, bq, Wk, bk, Wv, bv, Wo, bo):
        import jax, jax.numpy as jnp
        import numpy as np
        H = 16
        D_MODEL = 128
        DK = D_MODEL // H
        NEG = -1000000000.0

        def _split_heads(x, B, S):
            return x.reshape(B, S, H, DK).transpose(0, 2, 1, 3)
        B, S, D = q.shape
        qh = _split_heads(q @ Wq.T + bq, B, S)
        kh = _split_heads(k @ Wk.T + bk, B, S)
        vh = _split_heads(v @ Wv.T + bv, B, S)
        scores = jnp.einsum('bhqd,bhkd->bhqk', qh, kh) / np.sqrt(DK)
        scores = jnp.where(mask[:, None, :, :] == 0, NEG, scores)
        attn = jax.nn.softmax(scores, axis=-1)
        out = jnp.einsum('bhqk,bhkd->bhqd', attn, vh)
        out = out.transpose(0, 2, 1, 3).reshape(B, S, D)
        return out @ Wo.T + bo

    def _L0_ffn_ref(hidden_states, router_w, w_gate, w_up, w_down):
        import jax, jax.numpy as jnp
        import numpy as np
        JITTER_EPS = 0.01
        NEG_INF = -jnp.inf

        def sparsemixer_eval(scores, jitter_eps):
            m1 = jnp.max(scores, axis=-1, keepdims=True)
            ind1 = jnp.argmax(scores, axis=-1)
            factor1 = jnp.maximum(jnp.abs(scores), m1)
            mask1 = jax.lax.stop_gradient((m1 - scores) / factor1 > 2.0 * jitter_eps)
            gates1 = jax.nn.softmax(jnp.where(mask1, NEG_INF, scores), axis=-1)
            mult1 = jnp.take_along_axis(gates1, ind1[:, None], axis=-1)[:, 0]
            E = scores.shape[-1]
            onehot1 = ind1[:, None] == jnp.arange(E)[None, :]
            masked_scores = jnp.where(onehot1, NEG_INF, scores)
            m2 = jnp.max(masked_scores, axis=-1, keepdims=True)
            ind2 = jnp.argmax(masked_scores, axis=-1)
            factor2 = jnp.maximum(jnp.abs(scores), m2)
            mask2 = jax.lax.stop_gradient((m2 - scores) / factor2 > 2.0 * jitter_eps)
            gates2 = jax.nn.softmax(jnp.where(mask2, NEG_INF, masked_scores), axis=-1)
            mult2 = jnp.take_along_axis(gates2, ind2[:, None], axis=-1)[:, 0]
            multiplier = jnp.stack([mult1, mult2], axis=-1)
            selected = jnp.stack([ind1, ind2], axis=-1)
            return (multiplier, selected)
        B, S, H = hidden_states.shape
        E = router_w.shape[0]
        x = hidden_states.reshape(-1, H)
        T = x.shape[0]
        logits = x @ router_w.T
        routing_weights, selected = sparsemixer_eval(logits, JITTER_EPS)
        tok = jnp.arange(T)
        dense_w = jnp.zeros((T, E), dtype=x.dtype)
        dense_w = dense_w.at[tok, selected[:, 0]].add(routing_weights[:, 0])
        dense_w = dense_w.at[tok, selected[:, 1]].add(routing_weights[:, 1])
        out = jnp.zeros_like(x)
        for e in range(E):
            h = jax.nn.silu(x @ w_gate[e].T) * (x @ w_up[e].T)
            out = out + dense_w[:, e:e + 1] * (h @ w_down[e].T)
        return out.reshape(B, S, H)
    x = _layernorm(x + _L0_attn_ref(x, L0_attn_w_q, L0_attn_w_k, L0_attn_w_v, L0_attn_w_o), axis=-1)
    x = _layernorm(x + _L0_xattn_ref(x, ctx_1024, ctx_1024, mask_BxSxS2_ik1, L0_xattn_Wq, L0_xattn_bq, L0_xattn_Wk, L0_xattn_bk, L0_xattn_Wv, L0_xattn_bv, L0_xattn_Wo, L0_xattn_bo), axis=-1)
    x = _layernorm(x + _L0_ffn_ref(x, L0_ffn_router_w, L0_ffn_w_gate, L0_ffn_w_up, L0_ffn_w_down), axis=-1)
    return x

_drawn_inputs = setup_inputs


def setup_inputs(seed=0):
    import zlib

    import numpy as np

    out = dict(_drawn_inputs(seed))
    spreads = {'L0_xattn_bq': (0.0, 0.317),
     'L0_xattn_bk': (0.0, 0.8),
     'L0_xattn_bv': (0.0, 0.1),
     'L0_xattn_bo': (0.0, 0.1)}
    factors = {'L0_attn_w_q': 8.0,
     'L0_attn_w_k': 8.0,
     'L0_ffn_router_w': 5.755,
     'L0_ffn_w_gate': 4.933,
     'L0_ffn_w_up': 4.932,
     'L0_ffn_w_down': 4.94}
    for name, (base, spread) in spreads.items():
        noise = np.random.default_rng([zlib.crc32(name.encode()), seed]).standard_normal(out[name].shape)
        drawn = base * np.exp(spread * noise) if base else spread * noise
        out[name] = jnp.asarray(drawn.astype(out[name].dtype))
    for name, factor in factors.items():
        out[name] = (out[name] * factor).astype(out[name].dtype)
    return out
```

```python
from contextlib import ExitStack

import concourse.bass as bass
from concourse import mybir

F32 = mybir.dt.float32
F32R = mybir.dt.float32r
BF16 = mybir.dt.bfloat16
I32 = mybir.dt.int32
ALU = mybir.AluOpType
ACT = mybir.ActivationFunctionType
AX_X = mybir.AxisListType.X

P = 128
EPS = 1e-5
NEG = -1e30
JITTER2 = 0.02


def head_order(H):
    return [[8 * (g // 2) + g % 2 + 2 * i for i in range(4)] for g in range(H // 4)]


def spread(ap, axis, count):
    wide = ap.unsqueeze(axis)
    shape = list(wide.shape)
    shape[axis] = count
    return wide.broadcast_to(shape)


def build_decoder(nc, x, xT, ctxT, mask, wqT, wkT, wvT, woT, cwqT, cwkT, cwvT, cwoT, cbq, cbk, cbv, cbo,
                  routerT, gateT, upT, down, out):
    B, S, D = x.shape
    H, DQ = 16, 64
    HC, DC = 16, 8
    E = routerT.shape[1]
    F = gateT.shape[1] // E
    NG = H // 4
    FB = F // P
    KB = E * FB
    CH = 256
    NCH = B * S // CH
    TB = CH // P
    WP = E * F // B
    GROUPS = head_order(H)
    ORDER = [("s", 0), ("s", 1), ("c", 0), ("s", 2), ("c", 1), ("s", 3), ("c", 2), ("c", 3)]
    assert (S, D, H * DQ, HC * DC) == (P, P, 1024, D)

    with ExitStack() as ctx:
        def sb(name, shape, dt=F32):
            return ctx.enter_context(nc.sbuf_tensor(name, shape, dt))

        def sem(name):
            return ctx.enter_context(nc.semaphore(name))

        x_tok = sb("x_tok", [P, B, D])
        xT_all = sb("xT_all", [P, (B + 1) * S])
        ctxT_all = sb("ctxT_all", [P, B * S])
        mask_all = sb("mask_all", [P, B, S], I32)
        mask_add = sb("mask_add", [P, B, S], BF16)
        w_raw = sb("w_raw", [P, 3, H * DQ])
        w_hi = sb("w_hi", [P, 3, H * DQ], F32R)
        w_lo = sb("w_lo", [P, 3, H * DQ], F32R)
        wo_sb = sb("wo_sb", [P, H * DQ // P, D])
        cw = sb("cw", [P, 4, D])
        cb = sb("cb", [P, 2])
        cbrow = sb("cbrow", [P, 2, D])
        router_sb = sb("router_sb", [P, E])
        gu_raw = sb("gu_raw", [P, 2, E * F])
        gu_hi = sb("gu_hi", [P, 2, E * F], F32R)
        gu_lo = sb("gu_lo", [P, 2, E * F], F32R)
        down_sb = sb("down_sb", [P, KB, D])
        ident = sb("ident", [P, P])
        ident_bf = sb("ident_bf", [P, P], BF16)
        causal = sb("causal", [P, P], BF16)
        minus_half = sb("minus_half", [P, 2])
        x_hi = sb("x_hi", [P, S], F32R)
        x_lo = sb("x_lo", [P, S], F32R)
        qkT = sb("qkT", [P, 2, H // 2, S])
        v_sb = sb("v_sb", [P, H, DQ + 1])
        nmax_s = sb("nmax_s", [P, H])
        probs_s = sb("probs_s", [P, 2, 4, S])
        probsT_s = sb("probsT_s", [P, 2, 4, S])
        rsum_s = sb("rsum_s", [P, H])
        cat = sb("cat", [P, NG, 4, DQ])
        catT = sb("catT", [P, 2 * NG, S])
        res1 = sb("res1", [P, D])
        stat1 = sb("stat1", [P, 6])
        mv1 = sb("mv1", [P, 4])
        x1 = sb("x1", [P, D])
        ctx_cur = sb("ctx_cur", [P, S])
        mask_cur = sb("mask_cur", [P, S], BF16)
        x1T = sb("x1T", [P, S])
        x1bo = sb("x1bo", [P, D])
        k_f = sb("k_f", [P, S])
        q_f = sb("q_f", [P, S])
        k_hi = sb("k_hi", [P, S], F32R)
        k_lo = sb("k_lo", [P, S], F32R)
        q_hi = sb("q_hi", [P, S], F32R)
        q_lo = sb("q_lo", [P, S], F32R)
        k_stack = sb("k_stack", [P, 4, S], F32R)
        q_stack = sb("q_stack", [P, 4, S], F32R)
        spread_w = sb("spread_w", [P, 4, 4, P], F32R)
        cv = sb("cv", [P, HC, DC + 1])
        nmax_c = sb("nmax_c", [P, HC])
        probs_c = sb("probs_c", [P, 2, 4, S])
        probsT_c = sb("probsT_c", [P, 2, 4, S])
        rsum_c = sb("rsum_c", [P, HC])
        ccat = sb("ccat", [P, HC, DC])
        ccatT = sb("ccatT", [P, S])
        res2 = sb("res2", [P, D])
        stat2 = sb("stat2", [P, 6])
        mv2 = sb("mv2", [P, 4])
        x2_cur = sb("x2_cur", [P, D])
        x2T_cur = sb("x2T_cur", [P, S])
        x2_all = sb("x2_all", [P, B, D])
        x2T_hi = sb("x2T_hi", [P, B * S], F32R)
        x2T_lo = sb("x2T_lo", [P, B * S], F32R)
        logits = sb("logits", [P, B, E])
        r_m = sb("r_m", [P, 4, B])
        r_a = sb("r_a", [P, 6, B, E])
        pos = sb("pos", [P, B, E])
        dense_w = sb("dense_w", [P, B, E])
        w_cur = sb("w_cur", [P, TB, E])
        NS = 3
        NH = 4
        silu = sb("silu", [P, NS, CH])
        hid = sb("hid", [P, NH, CH])
        acc = sb("acc", [P, TB, D])
        stat3 = sb("stat3", [P, TB, 6])
        mv3 = sb("mv3", [P, TB, 4])
        y_out = sb("y_out", [P, TB, D])

        bank = [ctx.enter_context(nc.psum_tensor(f"bank{i}", [P, 512], F32)) for i in range(8)]
        SA, SB_, SC, SD, PTS, PTC, OS, OC = bank
        S_BANK = {("s", 0): SA, ("s", 1): SB_, ("s", 2): SA, ("s", 3): SB_,
                  ("c", 0): SC, ("c", 1): SD, ("c", 2): SC, ("c", 3): SD}
        GU_BANK = bank[0:4]
        Y_BANK = [bank[4], bank[6]]

        ld_xT, ld_wq, ld_wk, ld_wv, ld_x, ld_ctx, ld_mask, ld_wo, ld_cw, ld_gu, ld_down = [
            sem(f"ld_{n}") for n in "xT wq wk wv x ctx mask wo cw gu down".split()]
        spread_zero = sem("spread_zero")
        spread_ready = sem("spread_ready")
        stored = sem("stored")
        consts = sem("consts")
        mask_set = sem("mask_set")
        ones_set = sem("ones_set")
        w_hi_done = sem("w_hi_done")
        w_lo_done = sem("w_lo_done")
        gu_split = sem("gu_split")
        (x_split, qk_proj, qk_evac, v_proj, v_evac, rec_s, cat_norm, catT_ps, catT_evac, wo_s, res1_done, stat1_done,
         aggr1_done, var1_done, pow1_done, x1_ready) = [sem(n) for n in (
             "x_split qk_proj qk_evac v_proj v_evac rec_s cat_norm catT_ps catT_evac wo_s res1_done stat1_done "
             "aggr1_done var1_done pow1_done x1_ready").split()]
        scored = {k: sem(f"scored_{k}") for k in "sc"}
        maxed = {k: sem(f"maxed_{k}") for k in "sc"}
        exped = {k: sem(f"exped_{k}") for k in "sc"}
        turned = {k: sem(f"turned_{k}") for k in "sc"}
        turned_evac = {k: sem(f"turned_evac_{k}") for k in "sc"}
        mixed = {k: sem(f"mixed_{k}") for k in "sc"}
        (ctx_ready, mask_ready, ck_proj, cv_proj, ck_evac, cv_evac, x1T_ps, x1T_evac, cq_proj, cq_evac, k_hi_done,
         k_split, q_hi_done, q_split, x1bo_done, spread_k, spread_q, stack_k, stack_q, rec_c, ccat_norm) = [sem(n) for n in (
             "ctx_ready mask_ready ck_proj cv_proj ck_evac cv_evac x1T_ps x1T_evac cq_proj cq_evac k_hi_done "
             "k_split q_hi_done q_split x1bo_done spread_k spread_q stack_k stack_q rec_c ccat_norm").split()]
        (ccatT_ps, ccatT_evac, wo_c, res2_done, stat2_done, aggr2_done, var2_done, pow2_done, x2_ready, x2T_ps,
         x2T_evac, logit_ps, logit_evac, x2_split) = [sem(n) for n in (
             "ccatT_ps ccatT_evac wo_c res2_done stat2_done aggr2_done var2_done pow2_done x2_ready x2T_ps "
             "x2T_evac logit_ps logit_evac x2_split").split()]
        (r_step, r_exp_in, r_exp, dense_ready, w_cur_set, acc_set, gated, silued, hid_done, down_ps, combined, chained,
         stat3_done, aggr3_done, var3_done, pow3_done, y_ready) = [sem(n) for n in (
             "r_step r_exp_in r_exp dense_ready w_cur_set acc_set gated silued hid_done down_ps combined chained "
             "stat3_done aggr3_done var3_done pow3_done y_ready").split()]

        def wait(eng, s, value):
            if not isinstance(value, int) or value > 0:
                eng.wait_ge(s, value)

        def wait_apart(eng, *waits):
            waits = [(s, v if isinstance(v, int) else eng.snap(eng.to_reg(v), min_val=0)) for s, v in waits]
            eng.wait_ge(consts, 2)
            for s, v in waits:
                wait(eng, s, v)

        def slots(eng, slot):
            slot(0, True, False, False)
            slot(1, True, True, False)
            with eng.Fori(2, B) as n:
                slot(n, True, True, True)
            slot(B, False, True, True)
            slot(B + 1, False, False, True)

        block = ctx.enter_context(nc.Block())

        @block.sync
        def _(sp):
            sp.dma_start(xT_all[:, 0:B * S], xT).then_inc(ld_xT, 16)
            sp.dma_start(w_raw[:, 0, :], wqT).then_inc(ld_wq, 16)
            sp.dma_start(w_raw[:, 2, :], wvT).then_inc(ld_wv, 16)
            sp.dma_start(wo_sb[:], woT).then_inc(ld_wo, 16)
            for i, w in enumerate((cwqT, cwkT, cwvT, cwoT)):
                sp.dma_start(cw[:, i, :], w).then_inc(ld_cw, 16)
            sp.dma_start(cb[:, 0:1], cbq.rearrange("(d a) -> d a", a=1)).then_inc(ld_cw, 16)
            sp.dma_start(cb[:, 1:2], cbk.rearrange("(d a) -> d a", a=1)).then_inc(ld_cw, 16)
            sp.dma_start(cbrow[:, 0, :], cbv.rearrange("(a d) -> a d", a=1).broadcast_to([P, D])).then_inc(ld_cw, 16)
            sp.dma_start(cbrow[:, 1, :], cbo.rearrange("(a d) -> a d", a=1).broadcast_to([P, D])).then_inc(ld_cw, 16)
            sp.dma_start(router_sb[:], routerT).then_inc(ld_cw, 16)
            sp.dma_start(gu_raw[:, 0, :], gateT).then_inc(ld_gu, 16)
            sp.dma_start(gu_raw[:, 1, :], upT).then_inc(ld_gu, 16)
            sp.dma_start(down_sb[:], down).then_inc(ld_down, 16)

            for c in range(NCH):
                for tb in range(TB):
                    b = c * TB + tb
                    sp.wait_ge(y_ready, b + 1)
                    sp.dma_start(out[b], y_out[:, tb, :]).then_inc(stored, 16)
            sp.wait_ge(stored, 16 * B)

        @block.gpsimd
        def _(pool):
            def split_x(n):
                wait_apart(pool, (v_proj, 2 * n), (ld_xT, 16))
                src = xT_all[:, bass.ds(n * S, S)]
                pool.tensor_copy(x_hi[:], src).then_inc(x_split, 1)
                wait_apart(pool, (x_split, 2 * n + 1))
                pool.tensor_tensor(x_lo[:], src, x_hi[:].bitcast(F32), ALU.subtract).then_inc(x_split, 1)

            pool.memset(xT_all[:, B * S:], 0.0)
            pool.memset(ident[:], 0.0)
            pool.memset(ident_bf[:], 0.0)
            pool.memset(causal[:], 0.0)
            pool.memset(minus_half[:], -0.5)
            pool.memset(spread_w[:].rearrange("p a s c -> p (a s c)").bitcast(F32), 0.0).then_inc(spread_zero, 1)
            for e in range(E):
                last = pool.memset(pos[:, :, e:e + 1], float(e - E))
            last.then_inc(consts, 1)
            pool.wait_ge(consts, 1)
            pool.affine_select(out=ident[:], in_=ident[:], compare_op=ALU.not_equal, fill=1.0,
                               base=0, pattern=[[-1, P]], channel_multiplier=1)
            pool.affine_select(out=ident_bf[:], in_=ident_bf[:], compare_op=ALU.not_equal, fill=1.0,
                               base=0, pattern=[[-1, P]], channel_multiplier=1)
            pool.affine_select(out=causal[:], in_=causal[:], compare_op=ALU.is_ge, fill=NEG,
                               base=0, pattern=[[-1, P]], channel_multiplier=1).then_inc(consts, 1)
            split_x(0)

            pool.wait_ge(ld_mask, 16)
            pool.tensor_scalar(mask_add[:], mask_all[:], 0.0, NEG, ALU.is_equal, ALU.mult).then_inc(mask_set, 1)
            pool.wait_ge(spread_zero, 1)
            for part, rs in enumerate(((0, 2), (1, 3), (0, 1), (2, 3))):
                for s in range(4):
                    dst = spread_w[:, part, s, :].rearrange("p (j r i) -> p j r i", j=4, r=4)
                    src = ident[:].rearrange("p (j s i) -> p j s i", j=4, s=4)[:, :, s, :]
                    for r in rs:
                        last = pool.tensor_copy(dst[:, :, r, :], src)
            last.then_inc(spread_ready, 1)

            def slot(n, do_self, do_cross, do_post):
                m, l = n - 1, n - 2
                if do_cross:
                    wait_apart(pool, (ck_evac, m + 1), (spread_k, m))
                    pool.tensor_copy(k_hi[:], k_f[:]).then_inc(k_hi_done, 1)
                    pool.wait_ge(k_hi_done, m + 1)
                    pool.tensor_tensor(k_lo[:], k_f[:], k_hi[:].bitcast(F32), ALU.subtract).then_inc(k_split, 1)
                    pool.wait_ge(x1_ready, m + 1)
                    wait(pool, res2_done, m)
                    pool.tensor_tensor(x1bo[:], x1[:], cbrow[:, 1, :], ALU.add).then_inc(x1bo_done, 1)
                if do_post:
                    pool.wait_ge(var2_done, l + 1)
                    pool.tensor_tensor(mv2[:, 3:4], mv2[:, 2:3], minus_half[:, 0:1], ALU.pow).then_inc(pow2_done, 1)
                if do_cross:
                    wait_apart(pool, (cq_evac, m + 1), (spread_q, m))
                    pool.tensor_copy(q_hi[:], q_f[:]).then_inc(q_hi_done, 1)
                    pool.wait_ge(q_hi_done, m + 1)
                    pool.tensor_tensor(q_lo[:], q_f[:], q_hi[:].bitcast(F32), ALU.subtract).then_inc(q_split, 1)
                if do_post:
                    wait_apart(pool, (x2_ready, l + 1))
                    pool.tensor_copy(x2_all[:, bass.ds(l, 1), :].rearrange("p a d -> p (a d)"), x2_cur[:])
                    wait_apart(pool, (x2T_evac, l + 1))
                    hi, lo = x2T_hi[:, bass.ds(l * S, S)], x2T_lo[:, bass.ds(l * S, S)]
                    pool.tensor_copy(hi, x2T_cur[:]).then_inc(x2_split, 1)
                    wait_apart(pool, (x2_split, 2 * l + 1))
                    pool.tensor_tensor(lo, x2T_cur[:], hi.bitcast(F32), ALU.subtract).then_inc(x2_split, 1)
                if do_self:
                    pool.wait_ge(ld_gu, 32)
                    raw = gu_raw[:, :, bass.ds(n * WP, WP)]
                    hi, lo = gu_hi[:, :, bass.ds(n * WP, WP)], gu_lo[:, :, bass.ds(n * WP, WP)]
                    pool.tensor_copy(hi, raw).then_inc(gu_split, 1)
                    wait_apart(pool, (gu_split, 2 * n + 1))
                    pool.tensor_tensor(lo, raw, hi.bitcast(F32), ALU.subtract).then_inc(gu_split, 1)
                    split_x(n + 1)
                    wait_apart(pool, (cv_proj, n), (ld_ctx, 16))
                    pool.tensor_copy(ctx_cur[:], ctxT_all[:, bass.ds(n * S, S)]).then_inc(ctx_ready, 1)
                    wait_apart(pool, (scored["c"], NG * n), (mask_set, 1))
                    pool.tensor_copy(mask_cur[:], mask_add[:, bass.ds(n, 1), :].rearrange("p a d -> p (a d)"))\
                        .then_inc(mask_ready, 1)
                    pool.wait_ge(var1_done, n + 1)
                    pool.tensor_tensor(mv1[:, 3:4], mv1[:, 2:3], minus_half[:, 0:1], ALU.pow).then_inc(pow1_done, 1)

            slots(pool, slot)
            for c in range(NCH):
                for tb in range(TB):
                    pool.wait_ge(var3_done, c * TB + tb + 1)
                    pool.tensor_tensor(mv3[:, tb, 3:4], mv3[:, tb, 2:3], minus_half[:, 0:1],
                                       ALU.pow).then_inc(pow3_done, 1)

        @block.scalar
        def _(act):
            act.dma_start(w_raw[:, 1, :], wkT).then_inc(ld_wk, 16)
            act.dma_start(ctxT_all[:], ctxT).then_inc(ld_ctx, 16)
            act.dma_start(mask_all[:], mask.rearrange("b q t -> q b t")).then_inc(ld_mask, 16)
            act.dma_start(x_tok[:], x.rearrange("b q d -> q b d")).then_inc(ld_x, 16)
            for i, (ld, scale) in enumerate(((ld_wq, DQ ** -0.5), (ld_wk, 1.0), (ld_wv, 1.0))):
                act.wait_ge(ld, 16)
                act.activation(w_hi[:, i, :], w_raw[:, i, :], ACT.Copy, scale=scale).then_inc(w_hi_done, 1)

            def exp(kind, g, n):
                probs, nmax = (probs_s, nmax_s) if kind == "s" else (probs_c, nmax_c)
                b = S_BANK[kind, g]
                act.wait_ge(maxed[kind], NG * n + g + 1)
                wait(act, turned[kind], NG * n + g - 1)
                for i in range(4):
                    last = act.activation(probs[:, g % 2, i, :], b[:, i * S:(i + 1) * S], ACT.Exp,
                                          bias=nmax[:, 4 * g + i:4 * g + i + 1])
                last.then_inc(exped[kind], 1)

            def slot(n, do_self, do_cross, do_post):
                m, l = n - 1, n - 2

                def evac_qk(r):
                    act.wait_ge(qk_proj, 4 * n + r + 1)
                    act.copy(qkT[:, :, 2 * r:2 * r + 2, :].rearrange("p a b t -> p a (b t)"),
                             (SA, SB_)[r % 2][:].rearrange("p (a c) -> p a c", a=2)).then_inc(qk_evac, 1)

                if do_self:
                    evac_qk(0)
                    evac_qk(1)
                if do_cross:
                    act.wait_ge(ck_proj, m + 1)
                    act.wait_ge(ld_cw, 144)
                    wait(act, k_split, m)
                    act.activation(k_f[:], SC[:, 0:S], ACT.Identity, bias=cb[:, 1:2]).then_inc(ck_evac, 1)
                    act.wait_ge(x1T_ps, m + 1)
                    act.copy(x1T[:], PTC[:, 0:S]).then_inc(x1T_evac, 1)
                if do_self:
                    evac_qk(2)
                    evac_qk(3)
                    wait(act, mixed["s"], NG * n)
                    if isinstance(n, int) and n == 0:
                        act.wait_ge(ones_set, 1)
                    for c, b in enumerate((PTS, OS)):
                        act.wait_ge(v_proj, 2 * n + c + 1)
                        act.copy(v_sb[:, 8 * c:8 * c + 8, 0:DQ],
                                 b[:].rearrange("p (h v) -> p h v", v=DQ)).then_inc(v_evac, 1)
                if do_post:
                    act.wait_ge(x2T_ps, l + 1)
                    act.copy(x2T_cur[:], PTC[:, 0:S]).then_inc(x2T_evac, 1)
                if do_cross:
                    act.wait_ge(spread_q, m + 1)
                    wait(act, scored["c"], NG * m)
                    act.copy(q_stack[:].rearrange("p s t -> p (s t)"), SC[:]).then_inc(stack_q, 1)
                for kind, g in ORDER:
                    if kind == "s" and do_self:
                        exp(kind, g, n)
                    if kind == "c" and do_cross:
                        exp(kind, g, m)

            slots(act, slot)

            act.wait_ge(r_exp_in, 1)
            act.activation(r_a[:, 4:6].rearrange("p a b e -> p (a b e)"),
                           r_a[:, 0:2].rearrange("p a b e -> p (a b e)"), ACT.Exp).then_inc(r_exp, 1)
            for c in range(NCH):
                for k in range(KB):
                    i = c * KB + k
                    act.wait_ge(gated, i + 1)
                    wait(act, hid_done, i - NS + 1)
                    act.activation(silu[:, i % NS, :], GU_BANK[i % 4][:, 0:CH], ACT.Silu).then_inc(silued, 1)

        @block.vector
        def _(dve):
            dve.memset(v_sb[:], 1.0)
            dve.memset(cv[:], 1.0).then_inc(ones_set, 1)
            dve.wait_ge(ones_set, 1)
            for i, scale in enumerate((DQ ** -0.5, 1.0, 1.0)):
                dve.wait_ge(w_hi_done, i + 1)
                dve.scalar_tensor_tensor(out=w_lo[:, i, :], in0=w_raw[:, i, :], scalar=scale,
                                         in1=w_hi[:, i, :].bitcast(F32), op0=ALU.mult,
                                         op1=ALU.subtract).then_inc(w_lo_done, 1)

            def group_max(kind, g, n):
                nmax = nmax_s if kind == "s" else nmax_c
                dve.wait_ge(scored[kind], NG * n + g + 1)
                dve.tensor_reduce(nmax[:, 4 * g:4 * g + 4],
                                  S_BANK[kind, g][:].rearrange("p (h t) -> p h t", h=4), AX_X, ALU.max,
                                  negate=True).then_inc(maxed[kind], 1)

            def evac_turned(kind, g, n):
                dst, b = (probsT_s, PTS) if kind == "s" else (probsT_c, PTC)
                dve.wait_ge(turned[kind], NG * n + g + 1)
                wait(dve, mixed[kind], NG * n + g - 1)
                dve.tensor_copy(dst[:, g % 2].rearrange("p h t -> p (h t)"), b[:]).then_inc(turned_evac[kind], 1)

            def normalise_s(g, n):
                o = OS[:, 0:4 * (DQ + 1)].rearrange("p (h v) -> p h v", h=4)
                dve.wait_ge(mixed["s"], NG * n + g + 1)
                r = rsum_s[:, 4 * g:4 * g + 4]
                dve.reciprocal(r, o[:, :, DQ]).then_inc(rec_s, 1)
                dve.wait_ge(rec_s, NG * n + g + 1)
                dve.tensor_tensor(cat[:, g], o[:, :, 0:DQ], spread(r, 2, DQ),
                                  ALU.mult).then_inc(cat_norm, 1)

            def evac_catT(a, n):
                dve.wait_ge(catT_ps, 2 * n + a + 1)
                dve.tensor_copy(catT[:, 4 * a:4 * a + 4, :].rearrange("p c t -> p (c t)"), PTS[:]).then_inc(catT_evac, 1)

            def statistics(res, stat, mv, sems, n):
                res_done, stat_done, aggr_done, var_done = sems
                dve.wait_ge(res_done, n + 1)
                dve.bn_stats(stat, res).then_inc(stat_done, 1)
                wait_apart(dve, (stat_done, n + 1))
                dve.bn_aggr(mv[:, 0:2], stat).then_inc(aggr_done, 1)
                dve.wait_ge(aggr_done, n + 1)
                dve.tensor_scalar(mv[:, 2:3], mv[:, 1:2], EPS, None, ALU.add).then_inc(var_done, 1)

            def slot(n, do_self, do_cross, do_post):
                m, l = n - 1, n - 2
                if do_post:
                    dve.wait_ge(ccatT_ps, l + 1)
                    dve.tensor_copy(ccatT[:], PTC[:, 0:S]).then_inc(ccatT_evac, 1)
                if do_cross:
                    dve.wait_ge(cv_proj, m + 1)
                    dve.wait_ge(ld_cw, 144)
                    wait(dve, mixed["c"], NG * m)
                    dve.tensor_tensor(cv[:, :, 0:DC], SD[:, 0:D].rearrange("p (h v) -> p h v", v=DC),
                                      cbrow[:, 0, :].rearrange("p (h v) -> p h v", v=DC),
                                      ALU.add).then_inc(cv_evac, 1)
                if do_post:
                    dve.wait_ge(wo_c, l + 1)
                    dve.wait_ge(x1bo_done, l + 1)
                    dve.tensor_tensor(res2[:], OC[:, 0:D], x1bo[:], ALU.add).then_inc(res2_done, 1)
                    statistics(res2[:], stat2[:], mv2, (res2_done, stat2_done, aggr2_done, var2_done), l)
                if do_cross:
                    dve.wait_ge(cq_proj, m + 1)
                    wait(dve, q_split, m)
                    dve.tensor_scalar(q_f[:], OC[:, 0:S], cb[:, 0:1], DC ** -0.5, ALU.add, ALU.mult).then_inc(cq_evac, 1)
                    dve.wait_ge(spread_k, m + 1)
                    wait(dve, scored["c"], NG * m)
                    dve.tensor_copy(k_stack[:].rearrange("p s t -> p (s t)"), SD[:]).then_inc(stack_k, 1)
                if do_post:
                    dve.wait_ge(pow2_done, l + 1)
                    dve.tensor_scalar(x2_cur[:], res2[:], mv2[:, 0:1], mv2[:, 3:4], ALU.subtract,
                                      ALU.mult).then_inc(x2_ready, 1)
                    dve.wait_ge(logit_ps, l + 1)
                    dve.tensor_copy(logits[:, bass.ds(l, 1), :].rearrange("p a e -> p (a e)"),
                                    OC[:, 0:E]).then_inc(logit_evac, 1)

                order = [(k, g, n if k == "s" else m) for k, g in ORDER]
                live = {"s": do_self, "c": do_cross}

                def at(i, f):
                    if 0 <= i < len(order) and live[order[i][0]]:
                        f(*order[i])

                at(0, group_max)
                at(1, group_max)
                for i in range(len(order) + 1):
                    at(i + 2, group_max)
                    at(i, evac_turned)
                    if i >= 1 and order[i - 1][0] == "s" and do_self:
                        normalise_s(order[i - 1][1], n)
                    if i == 4 and do_self:
                        evac_catT(0, n)
                    if i == 7 and do_self:
                        evac_catT(1, n)
                if do_cross:
                    o = OC[:, 0:HC * (DC + 1)].rearrange("p (h v) -> p h v", h=HC)
                    dve.wait_ge(mixed["c"], NG * m + NG)
                    dve.reciprocal(rsum_c[:], o[:, :, DC]).then_inc(rec_c, 1)
                    dve.wait_ge(rec_c, m + 1)
                    dve.tensor_tensor(ccat[:], o[:, :, 0:DC], spread(rsum_c[:], 2, DC),
                                      ALU.mult).then_inc(ccat_norm, 1)
                if do_self:
                    dve.wait_ge(wo_s, n + 1)
                    dve.wait_ge(ld_x, 16)
                    dve.tensor_tensor(res1[:], OS[:, 0:D], x_tok[:, bass.ds(n, 1), :].rearrange("p a d -> p (a d)"),
                                      ALU.add).then_inc(res1_done, 1)
                    statistics(res1[:], stat1[:], mv1, (res1_done, stat1_done, aggr1_done, var1_done), n)
                    dve.wait_ge(pow1_done, n + 1)
                    wait(dve, x1T_ps, n)
                    wait(dve, x1bo_done, n)
                    dve.tensor_scalar(x1[:], res1[:], mv1[:, 0:1], mv1[:, 3:4], ALU.subtract,
                                      ALU.mult).then_inc(x1_ready, 1)

            slots(dve, slot)

            steps = [0]

            def step(ins):
                steps[0] += 1
                ins.then_inc(r_step, 1)
                dve.wait_ge(r_step, steps[0])

            s = logits[:]
            m1, i1, z1, z2 = (r_m[:, i, :] for i in range(4))
            d1, d2, t, u, e1, e2 = (r_a[:, i] for i in range(6))

            def wide(v):
                return spread(v, 2, E)

            tt = dve.tensor_tensor

            dve.wait_ge(logit_evac, B)

            def one_hot(dst, scores, top):
                step(tt(dst, scores, wide(top), ALU.is_equal))
                step(tt(dst, dst, pos[:], ALU.mult))
                step(dve.tensor_reduce(i1, dst, AX_X, ALU.min))
                step(tt(dst, pos[:], wide(i1), ALU.is_equal))

            def far(dst, diff, top):
                step(dve.scalar_tensor_tensor(out=dst, in0=s, scalar=-1.0, in1=s, op0=ALU.mult, op1=ALU.max))
                step(tt(dst, dst, wide(top), ALU.max))
                step(dve.scalar_tensor_tensor(out=dst, in0=dst, scalar=-JITTER2, in1=diff, op0=ALU.mult,
                                              op1=ALU.is_le))

            keep1 = sb("keep1", [P, B, E])
            keep2 = sb("keep2", [P, B, E])
            hot1 = sb("hot1", [P, B, E])
            hot2 = sb("hot2", [P, B, E])
            s2 = sb("s2", [P, B, E])
            step(dve.tensor_reduce(m1, s, AX_X, ALU.max))
            step(tt(d1, s, wide(m1), ALU.subtract))
            one_hot(hot1[:], s, m1)
            far(keep1[:], d1, m1)
            step(dve.scalar_tensor_tensor(out=s2[:], in0=hot1[:], scalar=NEG, in1=s, op0=ALU.mult, op1=ALU.add))
            step(dve.tensor_reduce(z1, s2[:], AX_X, ALU.max))
            step(tt(d2, s, wide(z1), ALU.subtract))
            far(keep2[:], d2, z1)
            step(tt(d2, s2[:], wide(z1), ALU.subtract))
            dve.engine_nop().then_inc(r_exp_in, 1)
            one_hot(hot2[:], s2[:], z1)
            dve.wait_ge(r_exp, 1)
            step(tt(e1, e1, keep1[:], ALU.mult))
            step(tt(e2, e2, keep2[:], ALU.mult))
            step(dve.tensor_reduce(z1, e1, AX_X, ALU.add))
            step(dve.tensor_reduce(z2, e2, AX_X, ALU.add))
            step(dve.reciprocal(z1, z1))
            step(dve.reciprocal(z2, z2))
            step(tt(hot1[:], hot1[:], wide(z1), ALU.mult))
            step(tt(hot2[:], hot2[:], wide(z2), ALU.mult))
            step(tt(dense_w[:], hot1[:], hot2[:], ALU.add))

            def hidden(i):
                dve.wait_ge(silued, i + 1)
                wait(dve, down_ps, (i // FB) - NH // FB + 1)
                dve.tensor_tensor(hid[:, i % NH, :], silu[:, i % NS, :], GU_BANK[i % 4][:, CH:2 * CH],
                                  ALU.mult).then_inc(hid_done, 1)

            def combine(c, e):
                ce = c * E + e
                dve.wait_ge(down_ps, ce + 1)
                for tb in range(TB):
                    b = c * TB + tb
                    if e == 0:
                        wait(dve, y_ready, b - TB + 1)
                    else:
                        dve.wait_ge(combined, (ce - 1) * TB + tb + 1)
                    dve.scalar_tensor_tensor(out=acc[:, tb, :], in0=Y_BANK[ce % 2][:, tb * P:(tb + 1) * P],
                                             scalar=dense_w[:, b, e:e + 1],
                                             in1=x2_all[:, b, :] if e == 0 else acc[:, tb, :],
                                             op0=ALU.mult, op1=ALU.add).then_inc(combined, 1)

            for c in range(NCH):
                for e in range(E):
                    for fb in range(FB):
                        hidden((c * E + e) * FB + fb)
                    if e >= 1:
                        combine(c, e - 1)
                combine(c, E - 1)
                for tb in range(TB):
                    b = c * TB + tb
                    dve.wait_ge(combined, (c * E + E - 1) * TB + tb + 1)
                    dve.bn_stats(stat3[:, tb, :], acc[:, tb, :]).then_inc(stat3_done, 1)
                    dve.wait_ge(stat3_done, b + 1)
                    dve.bn_aggr(mv3[:, tb, 0:2], stat3[:, tb, :]).then_inc(aggr3_done, 1)
                    dve.wait_ge(aggr3_done, b + 1)
                    dve.tensor_scalar(mv3[:, tb, 2:3], mv3[:, tb, 1:2], EPS, None, ALU.add).then_inc(var3_done, 1)
                for tb in range(TB):
                    b = c * TB + tb
                    dve.wait_ge(pow3_done, b + 1)
                    wait(dve, stored, 16 * (b - TB + 1) if b < TB else 16 * c * TB)
                    dve.tensor_scalar(y_out[:, tb, :], acc[:, tb, :], mv3[:, tb, 0:1], mv3[:, tb, 3:4],
                                      ALU.subtract, ALU.mult).then_inc(y_ready, 1)

        @block.tensor
        def _(pe):
            def split_product(dst, w, xs, start=True):
                (wh, wl), (xh, xl) = w, xs
                pe.matmul(dst, wh, xh, start=start, stop=False)
                pe.matmul(dst, wh, xl, start=False, stop=False)
                return pe.matmul(dst, wl, xh, start=False, stop=True)

            def score_s(g, n):
                b = S_BANK["s", g]
                if g < 2:
                    pe.wait_ge(qk_evac, 4 * n + 3 + g)
                else:
                    pe.wait_ge(exped["s"], NG * n + g - 1)
                pe.matmul(b[:], ident_bf[:], spread(causal[:], 1, 4), start=True, stop=False,
                          skip_group_check=True)
                for i, h in enumerate(GROUPS[g]):
                    rows = slice(64 * (h % 2), 64 * (h % 2) + 64)
                    last = pe.matmul(b[:, i * S:(i + 1) * S], qkT[rows, 0, h // 2, :], qkT[rows, 1, h // 2, :],
                                     start=False, stop=(i == 3), skip_group_check=True)
                last.then_inc(scored["s"], 1)

            def score_c(j, m):
                b = S_BANK["c", j]
                if j == 0:
                    pe.wait_ge(stack_q, m + 1)
                    pe.wait_ge(stack_k, m + 1)
                    pe.wait_ge(mask_ready, m + 1)
                elif j >= 2:
                    pe.wait_ge(exped["c"], NG * m + j - 1)
                pe.matmul(b[:], ident_bf[:], spread(mask_cur[:], 1, 4), start=True, stop=False,
                          skip_group_check=True)
                rows = slice(32 * j, 32 * j + 32)
                for i in range(4):
                    last = pe.matmul(b[:, i * S:(i + 1) * S], q_stack[rows, i, :], k_stack[rows, i, :],
                                     start=False, stop=(i == 3), skip_group_check=True)
                last.then_inc(scored["c"], 1)

            def spread_parts(b, which, parts, done):
                for s in range(4):
                    pe.matmul(b[:, s * S:(s + 1) * S], spread_w[:, 2 * which, s, :], parts[0][:], start=True, stop=False)
                    last = pe.matmul(b[:, s * S:(s + 1) * S], spread_w[:, 2 * which + 1, s, :], parts[1][:],
                                     start=False, stop=True)
                last.then_inc(done, 1)

            def turn(kind, g, n):
                probs, b = (probs_s, PTS) if kind == "s" else (probs_c, PTC)
                pe.wait_ge(exped[kind], NG * n + g + 1)
                if g:
                    pe.wait_ge(turned_evac[kind], NG * n + g)
                elif kind == "s":
                    pe.wait_ge(v_evac, 2 * n + 1)
                else:
                    pe.wait_ge(x1T_evac, n + 1)
                if kind == "s" and g == 3:
                    pe.wait_ge(catT_evac, 2 * n + 1)
                for i in range(4):
                    last = pe.transpose(b[:, i * S:(i + 1) * S], probs[:, g % 2, i, :], ident[:])
                last.then_inc(turned[kind], 1)

            def mix_s(g, n):
                pe.wait_ge(turned_evac["s"], NG * n + g + 1)
                if g == 0:
                    pe.wait_ge(v_evac, 2 * n + 2)
                else:
                    pe.wait_ge(cat_norm, NG * n + g)
                for i, h in enumerate(GROUPS[g]):
                    last = pe.matmul(OS[:, i * (DQ + 1):(i + 1) * (DQ + 1)], probsT_s[:, g % 2, i, :], v_sb[:, h, :],
                                     start=True, stop=True)
                last.then_inc(mixed["s"], 1)

            def mix_c(j, m):
                pe.wait_ge(turned_evac["c"], NG * m + j + 1)
                for i in range(4):
                    h = 4 * j + i
                    last = pe.matmul(OC[:, h * (DC + 1):(h + 1) * (DC + 1)], probsT_c[:, j % 2, i, :], cv[:, h, :],
                                     start=True, stop=True)
                last.then_inc(mixed["c"], 1)

            def turn_cat(a, n):
                pe.wait_ge(cat_norm, NG * n + 2 * a + 2)
                pe.wait_ge(turned_evac["s"], NG * n + (3 if a == 0 else 4))
                for i in range(4):
                    g, half = 2 * a + i // 2, i % 2
                    last = pe.transpose(PTS[:, i * P:(i + 1) * P],
                                        cat[:, g, 2 * half:2 * half + 2, :].rearrange("p h v -> p (h v)"), ident[:])
                last.then_inc(catT_ps, 1)

            def slot(n, do_self, do_cross, do_post):
                m, l = n - 1, n - 2
                first = isinstance(n, int) and n == 0

                def project_qk(r):
                    b = (SA, SB_)[r % 2]
                    if r == 0:
                        pe.wait_ge(x_split, 2 * n + 2)
                        if first:
                            pe.wait_ge(w_lo_done, 2)
                            pe.wait_ge(consts, 2)
                    if r < 2:
                        wait(pe, exped["s"], NG * (n - 1) + 3 + r)
                    else:
                        pe.wait_ge(qk_evac, 4 * n + r - 1)
                    for a in range(2):
                        for c in range(2):
                            p = 2 * r + c
                            cols = slice(p * P, (p + 1) * P)
                            last = split_product(b[:, (2 * a + c) * S:(2 * a + c + 1) * S],
                                                 (w_hi[:, a, cols], w_lo[:, a, cols]), (x_hi[:], x_lo[:]))
                    last.then_inc(qk_proj, 1)

                if do_self:
                    project_qk(0)
                if do_post:
                    pe.wait_ge(ccat_norm, l + 1)
                    pe.wait_ge(turned_evac["c"], NG * l + NG)
                    pe.transpose(PTC[:, 0:S], ccat[:].rearrange("p h v -> p (h v)"), ident[:]).then_inc(ccatT_ps, 1)
                if do_self:
                    project_qk(1)
                if do_cross:
                    pe.wait_ge(ctx_ready, m + 1)
                    wait(pe, exped["c"], NG * m)
                    pe.wait_ge(ld_cw, 144)
                    pe.matmul(SC[:, 0:S], cw[:, 1, :], ctx_cur[:], start=True, stop=True).then_inc(ck_proj, 1)
                    pe.matmul(SD[:, 0:D], ctx_cur[:], cw[:, 2, :], start=True, stop=True).then_inc(cv_proj, 1)
                if do_post:
                    pe.wait_ge(ccatT_evac, l + 1)
                    pe.matmul(OC[:, 0:D], ccatT[:], cw[:, 3, :], start=True, stop=True).then_inc(wo_c, 1)
                if do_cross:
                    pe.wait_ge(x1_ready, m + 1)
                    pe.transpose(PTC[:, 0:S], x1[:], ident[:]).then_inc(x1T_ps, 1)
                if do_self:
                    project_qk(2)
                if do_cross:
                    pe.wait_ge(x1T_evac, m + 1)
                    if do_post:
                        pe.wait_ge(res2_done, l + 1)
                    pe.matmul(OC[:, 0:S], cw[:, 0, :], x1T[:], start=True, stop=True).then_inc(cq_proj, 1)
                if do_self:
                    project_qk(3)
                if do_cross:
                    pe.wait_ge(k_split, m + 1)
                    pe.wait_ge(cv_evac, m + 1)
                    if not do_post:
                        pe.wait_ge(spread_ready, 1)
                    spread_parts(SD, 1, (k_hi, k_lo), spread_k)
                if do_self:
                    if first:
                        pe.wait_ge(w_lo_done, 3)
                    for c, b in enumerate((PTS, OS)):
                        if c == 0:
                            wait(pe, catT_evac, 2 * n)
                        else:
                            wait(pe, res1_done, n)
                        cols = slice(c * 512, (c + 1) * 512)
                        pe.matmul(b[:], x_hi[:], w_hi[:, 2, cols], start=True, stop=False)
                        pe.matmul(b[:], x_hi[:], w_lo[:, 2, cols], start=False, stop=False)
                        pe.matmul(b[:], x_lo[:], w_hi[:, 2, cols], start=False, stop=True).then_inc(v_proj, 1)
                if do_post:
                    pe.wait_ge(x2_ready, l + 1)
                    pe.transpose(PTC[:, 0:S], x2_cur[:], ident[:]).then_inc(x2T_ps, 1)

                order = [(k, g, n if k == "s" else m) for k, g in ORDER]
                live = {"s": do_self, "c": do_cross}

                def score(i):
                    if i < len(order):
                        kind, g, row = order[i]
                        if live[kind]:
                            (score_s if kind == "s" else score_c)(g, row)

                score(0)
                if do_cross:
                    pe.wait_ge(q_split, m + 1)
                    pe.wait_ge(ck_evac, m + 1)
                    spread_parts(SC, 0, (q_hi, q_lo), spread_q)
                if do_post:
                    pe.wait_ge(x2T_evac, l + 1)
                    if do_cross:
                        pe.wait_ge(cq_evac, m + 1)
                    pe.matmul(OC[:, 0:E], x2T_cur[:], router_sb[:], start=True, stop=True).then_inc(logit_ps, 1)
                score(1)
                for i in range(len(order) + 1):
                    score(i + 2)
                    if i < len(order) and live[order[i][0]]:
                        if order[i][:2] == ("c", 0) and do_post:
                            pe.wait_ge(x2T_evac, l + 1)
                        turn(*order[i])
                    if i >= 1 and live[order[i - 1][0]]:
                        kind, g, row = order[i - 1]
                        if (kind, g) == ("c", 0):
                            pe.wait_ge(cq_evac, m + 1)
                            if do_post:
                                pe.wait_ge(logit_evac, l + 1)
                        (mix_s if kind == "s" else mix_c)(g, row)
                    if i == 4 and do_self:
                        turn_cat(0, n)
                    if i == 7 and do_self:
                        turn_cat(1, n)
                if do_self:
                    pe.wait_ge(catT_evac, 2 * n + 2)
                    if first:
                        pe.wait_ge(ld_wo, 16)
                    for k in range(2 * NG):
                        last = pe.matmul(OS[:, 0:D], catT[:, k, :], wo_sb[:, k, :], start=(k == 0),
                                         stop=(k == 2 * NG - 1))
                    last.then_inc(wo_s, 1)

            slots(pe, slot)

            def gate_up(c, k):
                i = c * KB + k
                b = GU_BANK[i % 4]
                wait(pe, hid_done, i - 3)
                toks = slice(c * CH, (c + 1) * CH)
                cols = slice(k * P, (k + 1) * P)
                for a in range(2):
                    last = split_product(b[:, a * CH:(a + 1) * CH], (gu_hi[:, a, cols], gu_lo[:, a, cols]),
                                         (x2T_hi[:, toks], x2T_lo[:, toks]))
                last.then_inc(gated, 1)

            def down_product(c, e):
                ce = c * E + e
                pe.wait_ge(hid_done, (ce + 1) * FB)
                wait(pe, combined, TB * (ce - 1))
                for tb in range(TB):
                    for fb in range(FB):
                        i = ce * FB + fb
                        last = pe.matmul(Y_BANK[ce % 2][:, tb * P:(tb + 1) * P],
                                         hid[:, i % NH, tb * P:(tb + 1) * P], down_sb[:, e * FB + fb, :],
                                         start=(fb == 0), stop=(fb == FB - 1))
                last.then_inc(down_ps, 1)

            pe.wait_ge(x2_split, 2 * B)
            pe.wait_ge(gu_split, 2 * B)
            pe.wait_ge(ld_down, 16)
            pe.wait_ge(exped["c"], NG * B)
            for c in range(NCH):
                for e in range(E):
                    for fb in range(FB):
                        gate_up(c, e * FB + fb)
                    if c or e:
                        down_product(*((c, e - 1) if e else (c - 1, E - 1)))
            down_product(NCH - 1, E - 1)


def kernel(**inputs):
    import numpy as np
    import concourse.bacc as bacc
    from concourse.bass_utils import run_bass_kernel_spmd

    a = {k: np.asarray(v) for k, v in inputs.items()}
    B, S, D = a["x"].shape
    w_o = a["L0_attn_w_o"]
    H, DQ, _ = a["L0_attn_w_q"].shape
    E, F, _ = a["L0_ffn_w_gate"].shape
    order = [h for group in head_order(H) for h in group]
    wo_rows = w_o.T.reshape(H, DQ, D)[order].reshape(H * DQ // P, P, D)
    down = a["L0_ffn_w_down"].transpose(0, 2, 1).reshape(E * F // P, P, D)
    laid = {
        "x": a["x"],
        "xT": a["x"].transpose(2, 0, 1).reshape(D, B * S),
        "ctxT": a["ctx_1024"].transpose(2, 0, 1).reshape(D, B * S),
        "mask": a["mask_BxSxS2_ik1"],
        "wqT": a["L0_attn_w_q"].reshape(H * DQ, D).T,
        "wkT": a["L0_attn_w_k"].reshape(H * DQ, D).T,
        "wvT": a["L0_attn_w_v"].reshape(H * DQ, D).T,
        "woT": wo_rows.transpose(1, 0, 2),
        "cwqT": a["L0_xattn_Wq"].T,
        "cwkT": a["L0_xattn_Wk"].T,
        "cwvT": a["L0_xattn_Wv"].T,
        "cwoT": a["L0_xattn_Wo"].T,
        "cbq": a["L0_xattn_bq"],
        "cbk": a["L0_xattn_bk"],
        "cbv": a["L0_xattn_bv"],
        "cbo": a["L0_xattn_bo"],
        "routerT": a["L0_ffn_router_w"].T,
        "gateT": a["L0_ffn_w_gate"].reshape(E * F, D).T,
        "upT": a["L0_ffn_w_up"].reshape(E * F, D).T,
        "down": down.transpose(1, 0, 2),
    }
    laid = {k: np.ascontiguousarray(v) for k, v in laid.items()}
    nc = bacc.Bacc("TRN2", target_bir_lowering=False, num_devices=1)
    args = [nc.dram_tensor(f"in_{k}", v.shape, mybir.dt.from_np(v.dtype), kind="ExternalInput").ap()
            for k, v in laid.items()]
    out = nc.dram_tensor("out_0", (B, S, D), F32, kind="ExternalOutput").ap()
    build_decoder(nc, *args, out)
    r = run_bass_kernel_spmd(nc, [{f"in_{k}": v for k, v in laid.items()}], core_ids=[0])
    return r.results[0]["out_0"]
```

```python
from contextlib import ExitStack

import concourse.bass as bass
from concourse import mybir

F32 = mybir.dt.float32
F32R = mybir.dt.float32r
BF16 = mybir.dt.bfloat16
I32 = mybir.dt.int32
ALU = mybir.AluOpType
ACT = mybir.ActivationFunctionType
AX_X = mybir.AxisListType.X

P = 128
EPS = 1e-5
NEG = -1e30
JITTER2 = 0.02


def head_order(H):
    return [[8 * (g // 2) + g % 2 + 2 * i for i in range(4)] for g in range(H // 4)]


def spread(ap, axis, count):
    wide = ap.unsqueeze(axis)
    shape = list(wide.shape)
    shape[axis] = count
    return wide.broadcast_to(shape)


def build_decoder(nc, x, xT, ctxT, mask, wqT, wkT, wvT, woT, cwqT, cwkT, cwvT, cwoT, cbq, cbk, cbv, cbo,
                  parts, routerT, gateT, upT, down, out):
    B, S, D = x.shape
    H, DQ = 16, 64
    HC, DC = 16, 8
    E = routerT.shape[1]
    F = gateT.shape[1] // E
    NG = H // 4
    FB = F // P
    KB = E * FB
    CH = 256
    NCH = B * S // CH
    TB = CH // P
    WP = E * F // B
    GROUPS = head_order(H)
    ORDER = [("s", 0), ("s", 1), ("s", 2), ("c", 0), ("s", 3), ("c", 1), ("c", 2), ("c", 3)]
    AT_X2, AT_LOGITS, AT_CAT, AT_OUT = 1, 2, (3, 6), 7
    W_PARTS = [(0, slice(0, 512)), (1, slice(0, 512)), (0, slice(512, 1024)), (1, slice(512, 1024)), (2, slice(0, 1024))]
    W_SCALE = (DQ ** -0.5, 1.0, 1.0)
    WIDE = 10
    assert (S, D, H * DQ, HC * DC) == (P, P, 1024, D)

    with ExitStack() as ctx:
        def sb(name, shape, dt=F32):
            return ctx.enter_context(nc.sbuf_tensor(name, shape, dt))

        def sem(name):
            return ctx.enter_context(nc.semaphore(name))

        x_tok = sb("x_tok", [P, B, D])
        xT_all = sb("xT_all", [P, (B + 2) * S])
        ctxT_all = sb("ctxT_all", [P, (B + 2) * S])
        mask_add = sb("mask_add", [P, B, S], BF16)
        raw = sb("raw", [P, 2 * E * F])
        w_raw = raw[:, 0:3 * H * DQ].rearrange("p (a c) -> p a c", a=3)
        gu_raw = raw[:].rearrange("p (a c) -> p a c", a=2)
        w_hi = sb("w_hi", [P, 3, H * DQ], F32R)
        w_lo = sb("w_lo", [P, 3, H * DQ], F32R)
        wo_sb = sb("wo_sb", [P, H * DQ // P, D])
        cwv_sb = sb("cwv_sb", [P, D])
        cwo_sb = sb("cwo_sb", [P, D])
        cwq_sb = sb("cwq_sb", [P, 4, P])
        cwk_hi = sb("cwk_hi", [P, 4, P], F32R)
        cwk_lo = sb("cwk_lo", [P, 4, P], F32R)
        cb = sb("cb", [P, 2, 4])
        cbq_sb = sb("cbq_sb", [P, 4])
        part = sb("part", [P, 4])
        cbrow = sb("cbrow", [P, 2, D])
        router_sb = sb("router_sb", [P, E])
        gu_hi = sb("gu_hi", [P, 2, E * F], F32R)
        gu_lo = sb("gu_lo", [P, 2, E * F], F32R)
        down_sb = sb("down_sb", [P, KB, D])
        ident = sb("ident", [P, P])
        causal = sb("causal", [P, P], BF16)
        minus_half = sb("minus_half", [P, 2])
        x_hi = sb("x_hi", [P, 2 * S], F32R)
        x_lo = sb("x_lo", [P, 2 * S], F32R)
        qkT = sb("qkT", [P, 2, H // 2, 2 * S])
        v_sb = sb("v_sb", [P, H, DQ + 1])
        nmax_s = sb("nmax_s", [P, H])
        masked_s = sb("masked_s", [P, 2, 4, S])
        probs_s = sb("probs_s", [P, 2, 4, S])
        probsT_s = sb("probsT_s", [P, 2, 4, S])
        rsum_s = sb("rsum_s", [P, H])
        cat = sb("cat", [P, NG, 4, DQ])
        catT = sb("catT", [P, 2 * NG, S])
        res1 = sb("res1", [P, D])
        stat1 = sb("stat1", [P, 6])
        mv1 = sb("mv1", [P, 4])
        x1 = sb("x1", [P, D])
        ctx_cur = sb("ctx_cur", [P, 2 * S])
        ctx_hi = sb("ctx_hi", [P, 2 * S], F32R)
        ctx_lo = sb("ctx_lo", [P, 2 * S], F32R)
        mask_cur = sb("mask_cur", [P, S], BF16)
        x1T = sb("x1T", [P, S])
        x1bo = sb("x1bo", [P, D])
        k_f = sb("k_f", [P, 4, 2 * S])
        cwqk_raw = k_f[:].rearrange("p s t -> p (s t)").rearrange("p (a s c) -> p a s c", a=2, s=4)
        k_hi = sb("k_hi", [P, 4, 2 * S], F32R)
        q_f = sb("q_f", [P, 4, S])
        q_hi = sb("q_hi", [P, 4, S], F32R)
        k_stack = sb("k_stack", [P, 4, 2 * S], F32R)
        q_stack = sb("q_stack", [P, 4, S], F32R)
        cv = sb("cv", [P, 2 * HC + WIDE - 1, DC + 1])
        nmax_c = sb("nmax_c", [P, HC])
        masked_c = sb("masked_c", [P, 2, 4, S])
        mask_all = masked_c[:].rearrange("p a h t -> p (a h t)").bitcast(I32).rearrange("p (b t) -> p b t", b=B)
        probs_c = sb("probs_c", [P, 2, 4, S])
        probsT_c = sb("probsT_c", [P, 2, 4, S])
        rsum_c = sb("rsum_c", [P, HC])
        ccat = sb("ccat", [P, HC, DC])
        ccatT = sb("ccatT", [P, S])
        res2 = sb("res2", [P, D])
        stat2 = sb("stat2", [P, 6])
        mv2 = sb("mv2", [P, 4])
        x2_cur = sb("x2_cur", [P, D])
        x2T_cur = sb("x2T_cur", [P, S])
        x2_all = sb("x2_all", [P, B, D])
        x2T_hi = sb("x2T_hi", [P, B * S], F32R)
        x2T_lo = sb("x2T_lo", [P, B * S], F32R)
        logits = sb("logits", [P, B, E])
        r_m = sb("r_m", [P, 4, B])
        r_a = sb("r_a", [P, 6, B, E])
        pos = sb("pos", [P, B, E])
        dense_w = sb("dense_w", [P, B, E])
        w_cur = sb("w_cur", [P, TB, E])
        NS = 3
        NH = 4
        silu = probs_s[:].rearrange("p a h t -> p (a h t)")[:, 0:NS * CH].rearrange("p (a t) -> p a t", a=NS)
        hid = masked_s[:].rearrange("p a h t -> p (a h t)").rearrange("p (a t) -> p a t", a=NH)
        free_s = probsT_s[:].rearrange("p a h t -> p (a h t)")
        acc = free_s[:, 0:TB * D].rearrange("p (a d) -> p a d", a=TB)
        y_out = free_s[:, TB * D:2 * TB * D].rearrange("p (a d) -> p a d", a=TB)
        keep1, keep2, hot1, hot2, s2 = [
            free_s[:, 2 * TB * D + i * B * E:2 * TB * D + (i + 1) * B * E].rearrange("p (b e) -> p b e", b=B)
            for i in range(5)]
        stat3 = sb("stat3", [P, TB, 6])
        mv3 = sb("mv3", [P, TB, 4])

        bank = [ctx.enter_context(nc.psum_tensor(f"bank{i}", [P, 512], F32)) for i in range(8)]
        SA, SB_, SC, TA, TB_, TC, OS, OC = bank
        SCORES = (SA, SB_, SC)
        TURNED = (TA, TB_, TC)
        def k_banks(first):
            return (OC, SC) if first else (SC, TC)

        PLACE = {group: i for i, group in enumerate(ORDER)}
        GU_BANK = bank[0:4]
        Y_BANK = [bank[4], bank[6]]

        ld_xT, ld_xT_rest, ld_wq, ld_wk, ld_wv, ld_x, ld_ctx, ld_mask, ld_wo, ld_cw, ld_gu, ld_down = [
            sem(f"ld_{n}") for n in "xT xT_rest wq wk wv x ctx mask wo cw gu down".split()]
        cw_ready = sem("cw_ready")
        stored = sem("stored")
        consts = sem("consts")
        mask_set = sem("mask_set")
        ones_set = sem("ones_set")
        w_hi_done = sem("w_hi_done")
        w_lo_done = sem("w_lo_done")
        gu_split = sem("gu_split")
        (x_split, qk_proj, qk_evac, v_proj, v_evac, rec_s, cat_norm, catT_ps, catT_evac, wo_s, res1_done, stat1_done,
         aggr1_done, var1_done, pow1_done, x1_ready) = [sem(n) for n in (
             "x_split qk_proj qk_evac v_proj v_evac rec_s cat_norm catT_ps catT_evac wo_s res1_done stat1_done "
             "aggr1_done var1_done pow1_done x1_ready").split()]
        scored = {k: sem(f"scored_{k}") for k in "sc"}
        maxed = {k: sem(f"maxed_{k}") for k in "sc"}
        exped = {k: sem(f"exped_{k}") for k in "sc"}
        turned = {k: sem(f"turned_{k}") for k in "sc"}
        turned_evac = {k: sem(f"turned_evac_{k}") for k in "sc"}
        mixed = {k: sem(f"mixed_{k}") for k in "sc"}
        (ctx_ready, ctx_copied, mask_ready, ck_proj, cv_proj, ck_evac, cv_evac, x1T_ps, x1T_evac, cq_proj, cq_evac, k_hi_done,
         q_hi_done, x1bo_done, stack_k, stack_q, rec_c, ccat_norm) = [sem(n) for n in (
             "ctx_ready ctx_copied mask_ready ck_proj cv_proj ck_evac cv_evac x1T_ps x1T_evac cq_proj cq_evac k_hi_done "
             "q_hi_done x1bo_done stack_k stack_q rec_c ccat_norm").split()]
        (ccatT_ps, ccatT_evac, wo_c, res2_done, stat2_done, aggr2_done, var2_done, pow2_done, x2_ready, x2T_ps,
         x2T_evac, logit_ps, logit_evac, x2_split) = [sem(n) for n in (
             "ccatT_ps ccatT_evac wo_c res2_done stat2_done aggr2_done var2_done pow2_done x2_ready x2T_ps "
             "x2T_evac logit_ps logit_evac x2_split").split()]
        (r_step, r_exp_in, r_exp, dense_ready, w_cur_set, acc_set, gated, silued, hid_done, down_ps, combined, chained,
         stat3_done, aggr3_done, var3_done, pow3_done, y_ready) = [sem(n) for n in (
             "r_step r_exp_in r_exp dense_ready w_cur_set acc_set gated silued hid_done down_ps combined chained "
             "stat3_done aggr3_done var3_done pow3_done y_ready").split()]

        def wait(eng, s, value):
            if not isinstance(value, int) or value > 0:
                eng.wait_ge(s, value)

        def wait_apart(eng, *waits):
            waits = [(s, v if isinstance(v, int) else eng.snap(eng.to_reg(v), min_val=0)) for s, v in waits]
            eng.wait_ge(consts, 2)
            for s, v in waits:
                wait(eng, s, v)

        def slots(eng, slot):
            slot(0, 0, True, False, False)
            slot(1, 1, True, True, False)
            with eng.Fori(1, B // 2) as pair:
                slot(pair * 2, 0, True, True, True)
                slot(pair * 2 + 1, 1, True, True, True)
            slot(B, 0, False, True, True)
            slot(B + 1, 1, False, False, True)

        block = ctx.enter_context(nc.Block())

        @block.sync
        def _(sp):
            sp.dma_start(xT_all[:, 0:2 * S], xT[:, 0:2 * S]).then_inc(ld_xT, 16)
            sp.dma_start(w_raw[:, 0, :], wqT).then_inc(ld_wq, 16)
            sp.dma_start(w_raw[:, 2, :], wvT).then_inc(ld_wv, 16)
            sp.dma_start(cwqk_raw[:, 0], cwqT).then_inc(ld_cw, 16)
            sp.dma_start(cwqk_raw[:, 1], cwkT).then_inc(ld_cw, 16)
            sp.dma_start(cwv_sb[:], cwvT).then_inc(ld_cw, 16)
            sp.dma_start(cwo_sb[:], cwoT).then_inc(ld_cw, 16)
            sp.dma_start(cb[:, 0], cbq).then_inc(ld_cw, 16)
            sp.dma_start(cb[:, 1], cbk).then_inc(ld_cw, 16)
            sp.dma_start(part[:], parts).then_inc(ld_cw, 16)
            sp.dma_start(cbrow[:, 0, :], cbv.rearrange("(a d) -> a d", a=1).broadcast_to([P, D])).then_inc(ld_cw, 16)
            sp.dma_start(cbrow[:, 1, :], cbo.rearrange("(a d) -> a d", a=1).broadcast_to([P, D])).then_inc(ld_cw, 16)
            sp.dma_start(router_sb[:], routerT).then_inc(ld_cw, 16)
            sp.dma_start(wo_sb[:], woT).then_inc(ld_wo, 16)
            sp.wait_ge(w_lo_done, 5)
            sp.dma_start(gu_raw[:, 0, :], gateT).then_inc(ld_gu, 16)
            sp.dma_start(gu_raw[:, 1, :], upT).then_inc(ld_gu, 16)
            sp.dma_start(down_sb[:], down).then_inc(ld_down, 16)

            for c in range(NCH):
                for tb in range(TB):
                    b = c * TB + tb
                    sp.wait_ge(y_ready, b + 1)
                    sp.dma_start(out[b], y_out[:, tb, :]).then_inc(stored, 16)
            sp.wait_ge(stored, 16 * B)

        @block.gpsimd
        def _(pool):
            def split_x(n):
                wait_apart(pool, (v_proj, 2 * n), (ld_xT if isinstance(n, int) and n == 0 else ld_xT_rest, 16))
                src = xT_all[:, bass.ds(n * S, 2 * S)]
                pool.tensor_copy(x_hi[:], src).then_inc(x_split, 1)
                wait_apart(pool, (x_split, n + 1))
                pool.tensor_tensor(x_lo[:], src, x_hi[:].bitcast(F32), ALU.subtract).then_inc(x_split, 1)

            def split_ctx(n):
                wait_apart(pool, (ck_proj, n), (ld_ctx, 16))
                src = ctxT_all[:, bass.ds(n * S, 2 * S)]
                pool.tensor_copy(ctx_hi[:], src).then_inc(ctx_ready, 1)
                wait_apart(pool, (ctx_ready, n + 1))
                pool.tensor_tensor(ctx_lo[:], src, ctx_hi[:].bitcast(F32), ALU.subtract).then_inc(ctx_ready, 1)

            pool.memset(xT_all[:, B * S:], 0.0)
            pool.memset(ctxT_all[:, B * S:], 0.0)
            pool.memset(ident[:], 0.0)
            pool.memset(causal[:], 0.0)
            pool.memset(minus_half[:], -0.5)
            for e in range(E):
                last = pool.memset(pos[:, :, e:e + 1], float(e - E))
            last.then_inc(consts, 1)
            pool.wait_ge(consts, 1)
            pool.affine_select(out=ident[:], in_=ident[:], compare_op=ALU.not_equal, fill=1.0,
                               base=0, pattern=[[-1, P]], channel_multiplier=1)
            pool.affine_select(out=causal[:], in_=causal[:], compare_op=ALU.is_ge, fill=NEG,
                               base=0, pattern=[[-1, P]], channel_multiplier=1).then_inc(consts, 1)
            split_x(0)
            split_ctx(0)
            pool.wait_ge(ld_cw, 160)
            pool.tensor_scalar(cwq_sb[:], cwqk_raw[:, 0], DC ** -0.5, None, ALU.mult)
            pool.tensor_scalar(cbq_sb[:], cb[:, 0], DC ** -0.5, None, ALU.mult)
            pool.tensor_copy(cwk_hi[:], cwqk_raw[:, 1]).then_inc(cw_ready, 1)
            pool.wait_ge(cw_ready, 1)
            pool.tensor_tensor(cwk_lo[:], cwqk_raw[:, 1], cwk_hi[:].bitcast(F32), ALU.subtract).then_inc(cw_ready, 1)
            pool.wait_ge(ld_mask, 16)
            pool.tensor_scalar(mask_add[:], mask_all, 0.0, NEG, ALU.is_equal, ALU.mult).then_inc(mask_set, 1)

            def slot(n, odd, do_self, do_cross, do_post):
                m, l = n - 1, n - 2
                if do_cross:
                    pool.wait_ge(x1_ready, m + 1)
                    wait(pool, res2_done, m)
                    pool.tensor_tensor(x1bo[:], x1[:], cbrow[:, 1, :], ALU.add).then_inc(x1bo_done, 1)
                if do_post:
                    pool.wait_ge(var2_done, l + 1)
                    pool.tensor_tensor(mv2[:, 3:4], mv2[:, 2:3], minus_half[:, 0:1], ALU.pow).then_inc(pow2_done, 1)
                if do_self:
                    pool.wait_ge(ld_gu, 32)
                    raw = gu_raw[:, :, bass.ds(n * WP, WP)]
                    hi, lo = gu_hi[:, :, bass.ds(n * WP, WP)], gu_lo[:, :, bass.ds(n * WP, WP)]
                    pool.tensor_copy(hi, raw).then_inc(gu_split, 1)
                    wait_apart(pool, (gu_split, 2 * n + 1))
                    pool.tensor_tensor(lo, raw, hi.bitcast(F32), ALU.subtract).then_inc(gu_split, 1)
                    if odd:
                        split_x(n + 1)
                        split_ctx(n + 1)
                    else:
                        wait_apart(pool, (cv_proj, n))
                        pool.tensor_copy(ctx_cur[:], ctxT_all[:, bass.ds(n * S, 2 * S)]).then_inc(ctx_copied, 2)
                if do_post:
                    wait_apart(pool, (x2_ready, l + 1))
                    pool.tensor_copy(x2_all[:, bass.ds(l, 1), :].rearrange("p a d -> p (a d)"), x2_cur[:])
                    wait_apart(pool, (x2T_evac, l + 1))
                    hi, lo = x2T_hi[:, bass.ds(l * S, S)], x2T_lo[:, bass.ds(l * S, S)]
                    pool.tensor_copy(hi, x2T_cur[:]).then_inc(x2_split, 1)
                    wait_apart(pool, (x2_split, 2 * l + 1))
                    pool.tensor_tensor(lo, x2T_cur[:], hi.bitcast(F32), ALU.subtract).then_inc(x2_split, 1)
                if do_self:
                    wait_apart(pool, (maxed["c"], NG * n), (mask_set, 1))
                    pool.tensor_copy(mask_cur[:], mask_add[:, bass.ds(n, 1), :].rearrange("p a d -> p (a d)"))\
                        .then_inc(mask_ready, 1)
                    pool.wait_ge(var1_done, n + 1)
                    pool.tensor_tensor(mv1[:, 3:4], mv1[:, 2:3], minus_half[:, 0:1], ALU.pow).then_inc(pow1_done, 1)

            slots(pool, slot)
            for c in range(NCH):
                for tb in range(TB):
                    pool.wait_ge(var3_done, c * TB + tb + 1)
                    pool.tensor_tensor(mv3[:, tb, 3:4], mv3[:, tb, 2:3], minus_half[:, 0:1],
                                       ALU.pow).then_inc(pow3_done, 1)

        @block.scalar
        def _(act):
            act.dma_start(w_raw[:, 1, :], wkT).then_inc(ld_wk, 16)
            act.dma_start(ctxT_all[:, 0:B * S], ctxT).then_inc(ld_ctx, 16)
            act.dma_start(xT_all[:, 2 * S:B * S], xT[:, 2 * S:B * S]).then_inc(ld_xT_rest, 16)
            act.dma_start(mask_all, mask.rearrange("b q t -> q b t")).then_inc(ld_mask, 16)
            act.dma_start(x_tok[:], x.rearrange("b q d -> q b d")).then_inc(ld_x, 16)
            for i, cols in W_PARTS:
                act.wait_ge((ld_wq, ld_wk, ld_wv)[i], 16)
                act.activation(w_hi[:, i, cols], w_raw[:, i, cols], ACT.Copy, scale=W_SCALE[i]).then_inc(w_hi_done, 1)

            def exp(kind, g, n):
                masked, probs, nmax = (masked_s, probs_s, nmax_s) if kind == "s" else (masked_c, probs_c, nmax_c)
                act.wait_ge(maxed[kind], NG * n + g + 1)
                wait(act, turned[kind], NG * n + g - 1)
                for i in range(4):
                    last = act.activation(probs[:, g % 2, i, :], masked[:, g % 2, i, :], ACT.Exp, scale=-1.0,
                                          bias=nmax[:, 4 * g + i:4 * g + i + 1])
                last.then_inc(exped[kind], 1)

            def slot(n, odd, do_self, do_cross, do_post):
                m, l = n - 1, n - 2

                def evac_qk(p):
                    act.wait_ge(qk_proj, 4 * n + p + 1)
                    act.copy(qkT[:, :, p, :], (SA, SB_)[p % 2][:].rearrange("p (a c) -> p a c", a=2)).then_inc(qk_evac, 1)

                def evac_x1T():
                    act.wait_ge(x1T_ps, m + 1)
                    act.copy(x1T[:], TB_[:, 0:S]).then_inc(x1T_evac, 1)

                def round_q():
                    if do_cross:
                        act.wait_ge(cq_evac, m + 1)
                        wait(act, stack_q, m)
                        act.activation(q_hi[:], q_f[:], ACT.Copy, scale=part[:, 0:1]).then_inc(q_hi_done, 1)

                def evac_v(c, b):
                    act.wait_ge(v_proj, 2 * n + c + 1)
                    act.copy(v_sb[:, 8 * c:8 * c + 8, 0:DQ], b[:].rearrange("p (h v) -> p h v", v=DQ)).then_inc(v_evac, 1)

                order = [(k, g, n if k == "s" else m) for k, g in ORDER]
                live = {"s": do_self, "c": do_cross}

                def at(i):
                    if live[order[i][0]]:
                        exp(*order[i])

                first = isinstance(n, int) and n == 0

                def evac_k(a):
                    wait(act, stack_k, n)
                    if first:
                        act.wait_ge(cw_ready, 2)
                    act.wait_ge(ck_proj, n + a + 1)
                    for c in range(2):
                        s = 2 * a + c
                        last = act.activation(k_f[:, s, :], k_banks(first)[a][:, c * 2 * S:(c + 1) * 2 * S], ACT.Identity,
                                              bias=cb[:, 1, s:s + 1])
                    last.then_inc(ck_evac, 1)

                def round_k():
                    act.wait_ge(ck_evac, n + 2)
                    act.activation(k_hi[:], k_f[:], ACT.Copy, scale=part[:, 1:2]).then_inc(k_hi_done, 2)

                if do_self and not odd:
                    evac_qk(0)
                    evac_qk(1)
                    if not first:
                        evac_k(0)
                    evac_qk(2)
                    if not first:
                        evac_k(1)
                    evac_qk(3)
                    if do_cross:
                        evac_x1T()
                    for p in range(4, 7):
                        evac_qk(p)
                    round_q()
                    evac_qk(7)
                    at(0)
                elif do_cross:
                    at(0)
                    evac_x1T()
                    if not odd:
                        round_q()
                elif odd:
                    at(0)
                if do_self:
                    wait(act, mixed["s"], NG * n)
                    if first:
                        act.wait_ge(ones_set, 1)
                    evac_v(0, OS)
                    at(1)
                    if odd:
                        round_q()
                    evac_v(1, TC)
                    if first:
                        evac_k(0)
                        evac_k(1)
                if do_self and not odd:
                    round_k()
                for i in range(len(order) + 1):
                    if 2 <= i < len(order):
                        at(i)
                    if i and order[i - 1][0] == "c" and do_cross:
                        g = order[i - 1][1]
                        act.wait_ge(turned["c"], NG * m + g + 1)
                        wait(act, mixed["c"], NG * m + g - 1)
                        act.copy(probsT_c[:, g % 2].rearrange("p h t -> p (h t)"),
                                 TURNED[(i - 1) % 3][:]).then_inc(turned_evac["c"], 1)
                    if i == AT_X2 + 1 and do_post:
                        act.wait_ge(x2T_ps, l + 1)
                        act.copy(x2T_cur[:], OC[:, 0:S]).then_inc(x2T_evac, 1)

            slots(act, slot)

            act.wait_ge(r_exp_in, 1)
            act.activation(r_a[:, 4:6].rearrange("p a b e -> p (a b e)"),
                           r_a[:, 0:2].rearrange("p a b e -> p (a b e)"), ACT.Exp).then_inc(r_exp, 1)
            for c in range(NCH):
                for k in range(KB):
                    i = c * KB + k
                    act.wait_ge(gated, i + 1)
                    wait(act, hid_done, i - NS + 1)
                    act.activation(silu[:, i % NS, :], GU_BANK[i % 4][:, 0:CH], ACT.Silu).then_inc(silued, 1)

        @block.vector
        def _(dve):
            dve.memset(v_sb[:], 1.0)
            dve.memset(cv[:], 1.0).then_inc(ones_set, 1)
            dve.wait_ge(ones_set, 1)
            for done, (i, cols) in enumerate(W_PARTS):
                dve.wait_ge(w_hi_done, done + 1)
                dve.scalar_tensor_tensor(out=w_lo[:, i, cols], in0=w_raw[:, i, cols], scalar=W_SCALE[i],
                                         in1=w_hi[:, i, cols].bitcast(F32), op0=ALU.mult,
                                         op1=ALU.subtract).then_inc(w_lo_done, 1)

            def group_max(kind, g, n):
                masked, nmax, add = (masked_s, nmax_s, causal) if kind == "s" else (masked_c, nmax_c, mask_cur)
                waits = [(scored[kind], NG * n + g + 1), (exped[kind], NG * n + g - 1)]
                if kind == "c" and g == 0:
                    waits.append((mask_ready, n + 1))
                wait_apart(dve, *waits)
                for i in range(4):
                    last = dve.tensor_tensor_reduce(
                        out=masked[:, g % 2, i, :], in0=SCORES[PLACE[kind, g] % 3][:, i * S:(i + 1) * S], in1=add[:], scale=-1.0,
                        scalar=3e38, op0=ALU.add, op1=ALU.min, accum_out=nmax[:, 4 * g + i:4 * g + i + 1])
                last.then_inc(maxed[kind], 1)

            def evac_turned(kind, g, n):
                if kind == "c":
                    return
                dve.wait_ge(turned["s"], NG * n + g + 1)
                wait(dve, mixed["s"], NG * n + g - 1)
                dve.tensor_copy(probsT_s[:, g % 2].rearrange("p h t -> p (h t)"), TURNED[PLACE[kind, g] % 3][:])\
                    .then_inc(turned_evac["s"], 1)

            def normalise_s(g, n):
                o = OS[:, 0:4 * (DQ + 1)].rearrange("p (h v) -> p h v", h=4)
                dve.wait_ge(mixed["s"], NG * n + g + 1)
                r = rsum_s[:, 4 * g:4 * g + 4]
                dve.reciprocal(r, o[:, :, DQ]).then_inc(rec_s, 1)
                dve.wait_ge(rec_s, NG * n + g + 1)
                dve.tensor_tensor(cat[:, g], o[:, :, 0:DQ], spread(r, 2, DQ),
                                  ALU.mult).then_inc(cat_norm, 1)

            def evac_catT(a, n):
                dve.wait_ge(catT_ps, 2 * n + a + 1)
                dve.tensor_copy(catT[:, 4 * a:4 * a + 4, :].rearrange("p c t -> p (c t)"), TC[:]).then_inc(catT_evac, 1)

            def statistics(res, stat, mv, sems, n):
                res_done, stat_done, aggr_done, var_done = sems
                dve.wait_ge(res_done, n + 1)
                dve.bn_stats(stat, res).then_inc(stat_done, 1)
                wait_apart(dve, (stat_done, n + 1))
                dve.bn_aggr(mv[:, 0:2], stat).then_inc(aggr_done, 1)
                dve.wait_ge(aggr_done, n + 1)
                dve.tensor_scalar(mv[:, 2:3], mv[:, 1:2], EPS, None, ALU.add).then_inc(var_done, 1)

            def slot(n, odd, do_self, do_cross, do_post):
                m, l = n - 1, n - 2
                order = [(k, g, n if k == "s" else m) for k, g in ORDER]
                live = {"s": do_self, "c": do_cross}

                def at(i, f):
                    if 0 <= i < len(order) and live[order[i][0]]:
                        f(*order[i])

                def stack_of_q():
                    dve.wait_ge(q_hi_done, m + 1)
                    wait(dve, scored["c"], NG * m)
                    dve.scalar_tensor_tensor(out=q_stack[:], in0=q_f[:], scalar=part[:, 2:3], in1=q_hi[:].bitcast(F32),
                                             op0=ALU.mult, op1=ALU.add).then_inc(stack_q, 1)

                if odd:
                    at(0, group_max)
                if do_post:
                    dve.wait_ge(ccatT_ps, l + 1)
                    dve.tensor_copy(ccatT[:], TB_[:, 0:S]).then_inc(ccatT_evac, 1)
                if odd:
                    at(1, group_max)
                if do_post:
                    dve.wait_ge(wo_c, l + 1)
                    dve.wait_ge(x1bo_done, l + 1)
                    dve.tensor_tensor(res2[:], OC[:, 0:D], x1bo[:], ALU.add).then_inc(res2_done, 1)
                    statistics(res2[:], stat2[:], mv2, (res2_done, stat2_done, aggr2_done, var2_done), l)
                if do_cross:
                    if not do_post:
                        dve.wait_ge(cw_ready, 2)
                    dve.wait_ge(cq_proj, m + 1)
                    dve.tensor_tensor(q_f[:], SC[:].rearrange("p (s t) -> p s t", s=4), spread(cbq_sb[:], 2, S),
                                      ALU.add).then_inc(cq_evac, 1)
                if do_cross and odd:
                    dve.wait_ge(cv_proj, m + 2)
                    dve.wait_ge(ld_cw, 160)
                    wait(dve, mixed["c"], NG * m)
                    for a in range(2):
                        last = dve.tensor_tensor(cv[:, a * HC:(a + 1) * HC, 0:DC],
                                                 TB_[:, a * D:(a + 1) * D].rearrange("p (h v) -> p h v", v=DC),
                                                 cbrow[:, 0, :].rearrange("p (h v) -> p h v", v=DC), ALU.add)
                    last.then_inc(cv_evac, 2)
                if not odd:
                    at(0, group_max)
                    at(1, group_max)
                if do_cross:
                    stack_of_q()
                for i in range(len(order) + 1):
                    at(i, evac_turned)
                    at(i + 2, group_max)
                    if i == AT_X2 - 1 and do_post:
                        dve.wait_ge(pow2_done, l + 1)
                        dve.tensor_scalar(x2_cur[:], res2[:], mv2[:, 0:1], mv2[:, 3:4], ALU.subtract,
                                          ALU.mult).then_inc(x2_ready, 1)
                    if i >= 1 and order[i - 1][0] == "s" and do_self:
                        normalise_s(order[i - 1][1], n)
                    if i in AT_CAT and do_self:
                        evac_catT(AT_CAT.index(i), n)
                    if i == AT_LOGITS and do_post:
                        dve.wait_ge(logit_ps, l + 1)
                        dve.tensor_copy(logits[:, bass.ds(l, 1), :].rearrange("p a e -> p (a e)"),
                                        OC[:, 0:E]).then_inc(logit_evac, 1)
                if do_self and not odd:
                    dve.wait_ge(k_hi_done, n + 2)
                    wait(dve, scored["c"], NG * n)
                    dve.scalar_tensor_tensor(out=k_stack[:], in0=k_f[:], scalar=part[:, 3:4], in1=k_hi[:].bitcast(F32),
                                             op0=ALU.mult, op1=ALU.add).then_inc(stack_k, 2)
                if do_self:
                    dve.wait_ge(wo_s, n + 1)
                    dve.wait_ge(ld_x, 16)
                    dve.tensor_tensor(res1[:], OS[:, 0:D], x_tok[:, bass.ds(n, 1), :].rearrange("p a d -> p (a d)"),
                                      ALU.add).then_inc(res1_done, 1)
                    statistics(res1[:], stat1[:], mv1, (res1_done, stat1_done, aggr1_done, var1_done), n)
                if do_cross:
                    o = OC[:, 0:HC * (DC + 1)].rearrange("p (h v) -> p h v", h=HC)
                    dve.wait_ge(mixed["c"], NG * m + NG)
                    dve.reciprocal(rsum_c[:], o[:, :, DC]).then_inc(rec_c, 1)
                    dve.wait_ge(rec_c, m + 1)
                    dve.tensor_tensor(ccat[:], o[:, :, 0:DC], spread(rsum_c[:], 2, DC),
                                      ALU.mult).then_inc(ccat_norm, 1)
                if do_self:
                    dve.wait_ge(pow1_done, n + 1)
                    wait(dve, x1T_ps, n)
                    wait(dve, x1bo_done, n)
                    dve.tensor_scalar(x1[:], res1[:], mv1[:, 0:1], mv1[:, 3:4], ALU.subtract,
                                      ALU.mult).then_inc(x1_ready, 1)

            slots(dve, slot)

            steps = [0]

            def step(ins):
                steps[0] += 1
                ins.then_inc(r_step, 1)
                dve.wait_ge(r_step, steps[0])

            s = logits[:]
            m1, i1, z1, z2 = (r_m[:, i, :] for i in range(4))
            d1, d2, t, u, e1, e2 = (r_a[:, i] for i in range(6))

            def wide(v):
                return spread(v, 2, E)

            tt = dve.tensor_tensor

            dve.wait_ge(logit_evac, B)

            def one_hot(dst, scores, top):
                step(tt(dst, scores, wide(top), ALU.is_equal))
                step(tt(dst, dst, pos[:], ALU.mult))
                step(dve.tensor_reduce(i1, dst, AX_X, ALU.min))
                step(tt(dst, pos[:], wide(i1), ALU.is_equal))

            def far(dst, diff, top):
                step(dve.scalar_tensor_tensor(out=dst, in0=s, scalar=-1.0, in1=s, op0=ALU.mult, op1=ALU.max))
                step(tt(dst, dst, wide(top), ALU.max))
                step(dve.scalar_tensor_tensor(out=dst, in0=dst, scalar=-JITTER2, in1=diff, op0=ALU.mult,
                                              op1=ALU.is_le))

            step(dve.tensor_reduce(m1, s, AX_X, ALU.max))
            step(tt(d1, s, wide(m1), ALU.subtract))
            one_hot(hot1[:], s, m1)
            far(keep1[:], d1, m1)
            step(dve.scalar_tensor_tensor(out=s2[:], in0=hot1[:], scalar=NEG, in1=s, op0=ALU.mult, op1=ALU.add))
            step(dve.tensor_reduce(z1, s2[:], AX_X, ALU.max))
            step(tt(d2, s, wide(z1), ALU.subtract))
            far(keep2[:], d2, z1)
            step(tt(d2, s2[:], wide(z1), ALU.subtract))
            dve.engine_nop().then_inc(r_exp_in, 1)
            one_hot(hot2[:], s2[:], z1)
            dve.wait_ge(r_exp, 1)
            step(tt(e1, e1, keep1[:], ALU.mult))
            step(tt(e2, e2, keep2[:], ALU.mult))
            step(dve.tensor_reduce(z1, e1, AX_X, ALU.add))
            step(dve.tensor_reduce(z2, e2, AX_X, ALU.add))
            step(dve.reciprocal(z1, z1))
            step(dve.reciprocal(z2, z2))
            step(tt(hot1[:], hot1[:], wide(z1), ALU.mult))
            step(tt(hot2[:], hot2[:], wide(z2), ALU.mult))
            step(tt(dense_w[:], hot1[:], hot2[:], ALU.add))

            def hidden(i):
                dve.wait_ge(silued, i + 1)
                wait(dve, down_ps, (i // FB) - NH // FB + 1)
                dve.tensor_tensor(hid[:, i % NH, :], silu[:, i % NS, :], GU_BANK[i % 4][:, CH:2 * CH],
                                  ALU.mult).then_inc(hid_done, 1)

            def combine(c, e):
                ce = c * E + e
                dve.wait_ge(down_ps, ce + 1)
                for tb in range(TB):
                    b = c * TB + tb
                    if e == 0:
                        wait(dve, y_ready, b - TB + 1)
                    else:
                        dve.wait_ge(combined, (ce - 1) * TB + tb + 1)
                    dve.scalar_tensor_tensor(out=acc[:, tb, :], in0=Y_BANK[ce % 2][:, tb * P:(tb + 1) * P],
                                             scalar=dense_w[:, b, e:e + 1],
                                             in1=x2_all[:, b, :] if e == 0 else acc[:, tb, :],
                                             op0=ALU.mult, op1=ALU.add).then_inc(combined, 1)

            def statistics_of_y(c, tb):
                b = c * TB + tb
                dve.wait_ge(combined, (c * E + E - 1) * TB + tb + 1)
                dve.bn_stats(stat3[:, tb, :], acc[:, tb, :]).then_inc(stat3_done, 1)
                dve.wait_ge(stat3_done, b + 1)
                dve.bn_aggr(mv3[:, tb, 0:2], stat3[:, tb, :]).then_inc(aggr3_done, 1)
                dve.wait_ge(aggr3_done, b + 1)
                dve.tensor_scalar(mv3[:, tb, 2:3], mv3[:, tb, 1:2], EPS, None, ALU.add).then_inc(var3_done, 1)

            def normalise_y(c, tb):
                b = c * TB + tb
                dve.wait_ge(pow3_done, b + 1)
                wait(dve, stored, 16 * TB * c)
                dve.tensor_scalar(y_out[:, tb, :], acc[:, tb, :], mv3[:, tb, 0:1], mv3[:, tb, 3:4],
                                  ALU.subtract, ALU.mult).then_inc(y_ready, 1)

            for c in range(NCH + 1):
                for i in range(KB if c < NCH else TB + 2):
                    if c < NCH:
                        hidden(c * KB + i)
                    if c and i == 1:
                        combine(c - 1, E - 1)
                    if c and 2 <= i < 2 + TB:
                        statistics_of_y(c - 1, i - 2)
                    if c and i == 1 + TB:
                        for tb in range(TB):
                            normalise_y(c - 1, tb)
                    if c < NCH and i % FB == FB - 1 and i > FB:
                        combine(c, i // FB - 1)

        @block.tensor
        def _(pe):
            def split_product(dst, w, xs, start=True):
                (wh, wl), (xh, xl) = w, xs
                pe.matmul(dst, wh, xh, start=start, stop=False)
                pe.matmul(dst, wh, xl, start=False, stop=False)
                return pe.matmul(dst, wl, xh, start=False, stop=True)

            def keep_warm(times):
                for _ in range(times):
                    pe.matmul(OC[:], x_hi[:, 0:S], w_hi[:, 2, 0:512], start=True, stop=True)

            def score_s(g, n, half):
                b = SCORES[PLACE["s", g] % 3]
                if not half and g < 2:
                    pe.wait_ge(qk_evac, 4 * n + 7 + g)
                for i, h in enumerate(GROUPS[g]):
                    rows, toks = slice(64 * (h % 2), 64 * (h % 2) + 64), slice(half * S, (half + 1) * S)
                    last = pe.matmul(b[:, i * S:(i + 1) * S], qkT[rows, 0, h // 2, toks], qkT[rows, 1, h // 2, toks],
                                     start=True, stop=True)
                last.then_inc(scored["s"], 1)

            def score_c(j, m, half):
                b = SCORES[PLACE["c", j] % 3]
                if j == 0:
                    pe.wait_ge(stack_q, m + 1)
                    pe.wait_ge(stack_k, m + 2 - half)
                rows = slice(32 * j, 32 * j + 32)
                for i in range(4):
                    last = pe.matmul(b[:, i * S:(i + 1) * S], q_stack[rows, i, :],
                                     k_stack[rows, i, half * S:(half + 1) * S], start=True, stop=True)
                last.then_inc(scored["c"], 1)

            def turn(kind, g, n):
                probs = probs_s if kind == "s" else probs_c
                b = TURNED[PLACE[kind, g] % 3]
                pe.wait_ge(exped[kind], NG * n + g + 1)
                for i in range(4):
                    last = pe.transpose(b[:, i * S:(i + 1) * S], probs[:, g % 2, i, :], ident[:])
                last.then_inc(turned[kind], 1)

            def mix_s(g, n):
                pe.wait_ge(turned_evac["s"], NG * n + g + 1)
                if g == 0:
                    pe.wait_ge(v_evac, 2 * n + 2)
                else:
                    pe.wait_ge(cat_norm, NG * n + g)
                for i, h in enumerate(GROUPS[g]):
                    last = pe.matmul(OS[:, i * (DQ + 1):(i + 1) * (DQ + 1)], probsT_s[:, g % 2, i, :], v_sb[:, h, :],
                                     start=True, stop=True)
                last.then_inc(mixed["s"], 1)

            def mix_c(j, m, half):
                pe.wait_ge(turned_evac["c"], NG * m + j + 1)
                for i in range(4):
                    h = 4 * j + i
                    last = pe.matmul(OC[:, h * (DC + 1):(h + WIDE) * (DC + 1)], probsT_c[:, j % 2, i, :],
                                     cv[:, half * HC + h:half * HC + h + WIDE, :].rearrange("p h v -> p (h v)"),
                                     start=True, stop=True)
                last.then_inc(mixed["c"], 1)

            def turn_cat(a, n):
                pe.wait_ge(cat_norm, NG * n + 2 * a + 2)
                for i in range(4):
                    g, half = 2 * a + i // 2, i % 2
                    last = pe.transpose(TC[:, i * P:(i + 1) * P],
                                        cat[:, g, 2 * half:2 * half + 2, :].rearrange("p h v -> p (h v)"), ident[:])
                last.then_inc(catT_ps, 1)

            def slot(n, odd, do_self, do_cross, do_post):
                m, l = n - 1, n - 2
                first = isinstance(n, int) and n == 0

                def project_qk(p):
                    b = (SA, SB_)[p % 2]
                    if p == 0:
                        pe.wait_ge(x_split, n + 2)
                        if first:
                            pe.wait_ge(consts, 2)
                    if first and p in (0, 4):
                        pe.wait_ge(w_lo_done, 2 if p == 0 else 4)
                    if p >= 2:
                        pe.wait_ge(qk_evac, 4 * n + p - 1)
                    cols = slice(p * P, (p + 1) * P)
                    for a in range(2):
                        last = split_product(b[:, a * 2 * S:(a + 1) * 2 * S], (w_hi[:, a, cols], w_lo[:, a, cols]),
                                             (x_hi[:], x_lo[:]))
                    last.then_inc(qk_proj, 1)

                def project_v(c):
                    b = (OS, TC)[c]
                    if first:
                        pe.wait_ge(w_lo_done, 5)
                    if c == 0:
                        wait(pe, res1_done, n)
                    elif not odd and not first:
                        pe.wait_ge(ck_evac, n + 2)
                    cols, toks = slice(c * 512, (c + 1) * 512), slice(odd * S, (odd + 1) * S)
                    pe.matmul(b[:], x_hi[:, toks], w_hi[:, 2, cols], start=True, stop=False)
                    pe.matmul(b[:], x_hi[:, toks], w_lo[:, 2, cols], start=False, stop=False)
                    pe.matmul(b[:], x_lo[:, toks], w_hi[:, 2, cols], start=False, stop=True).then_inc(v_proj, 1)

                def turn_ccat():
                    pe.wait_ge(ccat_norm, l + 1)
                    pe.transpose(TB_[:, 0:S], ccat[:].rearrange("p h v -> p (h v)"), ident[:]).then_inc(ccatT_ps, 1)

                def project_out_c():
                    pe.wait_ge(ccatT_evac, l + 1)
                    pe.matmul(OC[:, 0:D], ccatT[:], cwo_sb[:], start=True, stop=True).then_inc(wo_c, 1)

                def turn_x1():
                    pe.wait_ge(x1_ready, m + 1)
                    if do_post:
                        pe.wait_ge(ccatT_evac, l + 1)
                    pe.transpose(TB_[:, 0:S], x1[:], ident[:]).then_inc(x1T_ps, 1)

                def turn_x2():
                    pe.wait_ge(x2_ready, l + 1)
                    pe.transpose(OC[:, 0:S], x2_cur[:], ident[:]).then_inc(x2T_ps, 1)

                def project_kc(a):
                    b = k_banks(first)[a]
                    pe.wait_ge(ctx_ready, n + 2)
                    if first:
                        pe.wait_ge(cw_ready, 2)
                    for c in range(2):
                        s = 2 * a + c
                        last = split_product(b[:, c * 2 * S:(c + 1) * 2 * S], (cwk_hi[:, s, :], cwk_lo[:, s, :]),
                                             (ctx_hi[:], ctx_lo[:]))
                    last.then_inc(ck_proj, 1)

                def project_vc():
                    pe.wait_ge(x1T_evac, m + 1)
                    pe.wait_ge(ctx_copied, m + 2)
                    for a in range(2):
                        last = pe.matmul(TB_[:, a * D:(a + 1) * D], ctx_cur[:, a * S:(a + 1) * S], cwv_sb[:], start=True,
                                         stop=True)
                    last.then_inc(cv_proj, 2)

                def project_qc():
                    pe.wait_ge(x1T_evac, m + 1)
                    if do_self and not odd:
                        pe.wait_ge(ck_evac, n + 1)
                    for s in range(4):
                        last = pe.matmul(SC[:, s * S:(s + 1) * S], cwq_sb[:, s, :], x1T[:], start=True, stop=True)
                    last.then_inc(cq_proj, 1)

                order = [(k, g, n if k == "s" else m) for k, g in ORDER]
                live = {"s": do_self, "c": do_cross}

                def score(i):
                    if i < len(order):
                        kind, g, row = order[i]
                        if i == 2 and do_cross:
                            pe.wait_ge(cq_evac, m + 1)
                        if live[kind]:
                            (score_s if kind == "s" else score_c)(g, row, odd if kind == "s" else 1 - odd)

                if not odd:
                    if do_self:
                        project_qk(0)
                        project_qk(1)
                        if not first:
                            project_kc(0)
                    if do_post:
                        turn_ccat()
                    if do_self:
                        project_qk(2)
                        if not first:
                            project_kc(1)
                    if do_post:
                        project_out_c()
                    if do_self:
                        project_qk(3)
                    if do_cross:
                        turn_x1()
                    if do_self:
                        project_qk(4)
                    if do_cross:
                        project_qc()
                    if do_self:
                        project_qk(5)
                        project_qk(6)
                        project_qk(7)
                    score(0)
                    score(1)
                    if do_self:
                        project_v(0)
                        project_v(1)
                        if first:
                            project_kc(0)
                            project_kc(1)
                            pe.wait_ge(ck_evac, 2)
                else:
                    score(0)
                    score(1)
                    if do_post:
                        turn_ccat()
                    if do_self:
                        project_v(0)
                    if do_post:
                        project_out_c()
                    if do_cross:
                        turn_x1()
                    if do_self:
                        project_v(1)
                    if do_cross:
                        project_qc()
                        project_vc()
                for i in range(len(order) + 1):
                    score(i + 2)
                    if not do_cross and i < len(order) and live[order[i][0]]:
                        keep_warm(5)
                    if i < len(order) and live[order[i][0]]:
                        if i == 1 and do_cross:
                            pe.wait_ge(x1T_evac, m + 1)
                            if odd:
                                pe.wait_ge(cv_evac, m + 2)
                        if i == 2 and do_self:
                            pe.wait_ge(v_evac, 2 * n + 2)
                        if i == 5 and do_self:
                            pe.wait_ge(catT_evac, 2 * n + 1)
                        turn(*order[i])
                    if i >= 1 and live[order[i - 1][0]]:
                        kind, g, row = order[i - 1]
                        if (kind, g) == ("c", 0) and do_post:
                            pe.wait_ge(logit_evac, l + 1)
                        if kind == "s":
                            mix_s(g, row)
                        else:
                            mix_c(g, row, 1 - odd)
                    if i in AT_CAT and do_self:
                        turn_cat(AT_CAT.index(i), n)
                    if i == AT_X2 and do_post:
                        turn_x2()
                    if i == AT_LOGITS and do_post:
                        pe.wait_ge(x2T_evac, l + 1)
                        pe.matmul(OC[:, 0:E], x2T_cur[:], router_sb[:], start=True, stop=True).then_inc(logit_ps, 1)
                    if i == AT_OUT and do_self:
                        pe.wait_ge(catT_evac, 2 * n + 2)
                        if first:
                            pe.wait_ge(ld_wo, 16)
                        for k in range(2 * NG):
                            last = pe.matmul(OS[:, 0:D], catT[:, k, :], wo_sb[:, k, :], start=(k == 0),
                                             stop=(k == 2 * NG - 1))
                        last.then_inc(wo_s, 1)

            slots(pe, slot)

            def gate_up(c, k):
                i = c * KB + k
                b = GU_BANK[i % 4]
                wait(pe, hid_done, i - 3)
                toks = slice(c * CH, (c + 1) * CH)
                cols = slice(k * P, (k + 1) * P)
                for a in range(2):
                    last = split_product(b[:, a * CH:(a + 1) * CH], (gu_hi[:, a, cols], gu_lo[:, a, cols]),
                                         (x2T_hi[:, toks], x2T_lo[:, toks]))
                last.then_inc(gated, 1)

            def down_product(c, e):
                ce = c * E + e
                pe.wait_ge(hid_done, (ce + 1) * FB)
                wait(pe, combined, TB * (ce - 1))
                for tb in range(TB):
                    for fb in range(FB):
                        i = ce * FB + fb
                        last = pe.matmul(Y_BANK[ce % 2][:, tb * P:(tb + 1) * P],
                                         hid[:, i % NH, tb * P:(tb + 1) * P], down_sb[:, e * FB + fb, :],
                                         start=(fb == 0), stop=(fb == FB - 1))
                last.then_inc(down_ps, 1)

            pe.wait_ge(x2_split, 2 * B)
            pe.wait_ge(gu_split, 2 * B)
            pe.wait_ge(ld_down, 16)
            pe.wait_ge(exped["c"], NG * B)
            for c in range(NCH):
                for e in range(E):
                    for fb in range(FB):
                        gate_up(c, e * FB + fb)
                    if c or e:
                        down_product(*((c, e - 1) if e else (c - 1, E - 1)))
            down_product(NCH - 1, E - 1)


def kernel(**inputs):
    import numpy as np
    import concourse.bacc as bacc
    from concourse.bass_utils import run_bass_kernel_spmd

    a = {k: np.asarray(v) for k, v in inputs.items()}
    B, S, D = a["x"].shape
    w_o = a["L0_attn_w_o"]
    H, DQ, _ = a["L0_attn_w_q"].shape
    E, F, _ = a["L0_ffn_w_gate"].shape
    order = [h for group in head_order(H) for h in group]
    wo_rows = w_o.T.reshape(H, DQ, D)[order].reshape(H * DQ // P, P, D)
    down = a["L0_ffn_w_down"].transpose(0, 2, 1).reshape(E * F // P, P, D)
    row = np.arange(P)
    stack = 8 * (4 * (row // 32) + np.arange(4)[:, None]) + row % 8
    r = row % 32 // 8
    lower = np.stack([r % 2, r // 2], axis=1).astype(np.float32)
    laid = {
        "x": a["x"],
        "xT": a["x"].transpose(2, 0, 1).reshape(D, B * S),
        "ctxT": a["ctx_1024"].transpose(2, 0, 1).reshape(D, B * S),
        "mask": a["mask_BxSxS2_ik1"],
        "wqT": a["L0_attn_w_q"].reshape(H * DQ, D).T,
        "wkT": a["L0_attn_w_k"].reshape(H * DQ, D).T,
        "wvT": a["L0_attn_w_v"].reshape(H * DQ, D).T,
        "woT": wo_rows.transpose(1, 0, 2),
        "cwqT": a["L0_xattn_Wq"][stack].transpose(2, 0, 1),
        "cwkT": a["L0_xattn_Wk"][stack].transpose(2, 0, 1),
        "cwvT": a["L0_xattn_Wv"].T,
        "cwoT": a["L0_xattn_Wo"].T,
        "cbq": a["L0_xattn_bq"][stack].T,
        "cbk": a["L0_xattn_bk"][stack].T,
        "cbv": a["L0_xattn_bv"],
        "cbo": a["L0_xattn_bo"],
        "parts": np.concatenate([1 - 2 * lower, lower], axis=1),
        "routerT": a["L0_ffn_router_w"].T,
        "gateT": a["L0_ffn_w_gate"].reshape(E * F, D).T,
        "upT": a["L0_ffn_w_up"].reshape(E * F, D).T,
        "down": down.transpose(1, 0, 2),
    }
    laid = {k: np.ascontiguousarray(v) for k, v in laid.items()}
    nc = bacc.Bacc("TRN2", target_bir_lowering=False, num_devices=1)
    args = [nc.dram_tensor(f"in_{k}", v.shape, mybir.dt.from_np(v.dtype), kind="ExternalInput").ap()
            for k, v in laid.items()]
    out = nc.dram_tensor("out_0", (B, S, D), F32, kind="ExternalOutput").ap()
    build_decoder(nc, *args, out)
    r = run_bass_kernel_spmd(nc, [{f"in_{k}": v for k, v in laid.items()}], core_ids=[0])
    return r.results[0]["out_0"]
```

```python
from contextlib import ExitStack

import concourse.bass as bass
from concourse import mybir

F32 = mybir.dt.float32
F32R = mybir.dt.float32r
BF16 = mybir.dt.bfloat16
I32 = mybir.dt.int32
ALU = mybir.AluOpType
ACT = mybir.ActivationFunctionType
AX_X = mybir.AxisListType.X

P = 128
EPS = 1e-5
NEG = -1e30
JITTER2 = 0.02


def head_order(H):
    return [[8 * (g // 2) + g % 2 + 2 * i for i in range(4)] for g in range(H // 4)]


def spread(ap, axis, count):
    wide = ap.unsqueeze(axis)
    shape = list(wide.shape)
    shape[axis] = count
    return wide.broadcast_to(shape)


def build_decoder(nc, x, xT, ctxT, mask, wqT, wkT, wvT, woT, cwqT, cwkT, cwvT, cwoT, cbq, cbk, cbv, cbo,
                  parts, routerT, gateT, upT, down, out):
    B, S, D = x.shape
    H, DQ = 16, 64
    HC, DC = 16, 8
    E = routerT.shape[1]
    F = gateT.shape[1] // E
    NG = H // 4
    FB = F // P
    KB = E * FB
    CH = 256
    NCH = B * S // CH
    TB = CH // P
    WP = E * F // B
    GROUPS = head_order(H)
    ORDER = [("s", 0), ("s", 1), ("s", 2), ("c", 0), ("s", 3), ("c", 1), ("c", 2), ("c", 3)]
    CROSS_ONLY = [("c", j) for j in range(4)]
    AT_X2, AT_LOGITS, AT_CAT, AT_OUT = 1, 2, (3, 6), 7
    AT_K_FIRST = (0, 2)
    AT_X2_LAST, AT_LOGITS_LAST = 0, 0
    FILL = {(B, "start"): [0, 1], (B, "ccat"): [2], (B, "out"): [3], (B, "x1"): [4], (B, "q"): [5], (B, 0): [6, 7],
            (B, 1): [8], (B, 2): [9], (B, 3): [10], (B, 4): [11, 12, 13], (B + 1, "ccat"): [14],
            (B + 1, "out"): [15, 16, 17, 18], (B + 1, 0): [19, 20]}
    NFILL = 21
    assert sum(FILL.values(), []) == list(range(NFILL))

    def fill(n, place, work):
        for i in FILL.get((n, place), ()) if isinstance(n, int) else ():
            work(i)

    W_PARTS = [(0, slice(0, 512)), (1, slice(0, 512)), (0, slice(512, 1024)), (1, slice(512, 1024)), (2, slice(0, 1024))]
    W_SCALE = (DQ ** -0.5, 1.0, 1.0)
    WIDE = 10
    assert (S, D, H * DQ, HC * DC) == (P, P, 1024, D)

    with ExitStack() as ctx:
        def sb(name, shape, dt=F32):
            return ctx.enter_context(nc.sbuf_tensor(name, shape, dt))

        def sem(name):
            return ctx.enter_context(nc.semaphore(name))

        x_tok = sb("x_tok", [P, B, D])
        xT_all = sb("xT_all", [P, (B + 2) * S])
        ctxT_all = sb("ctxT_all", [P, (B + 2) * S])
        mask_add = sb("mask_add", [P, B, S], BF16)
        raw = sb("raw", [P, 2 * E * F])
        w_raw = raw[:, 0:3 * H * DQ].rearrange("p (a c) -> p a c", a=3)
        gu_raw = raw[:].rearrange("p (a c) -> p a c", a=2)
        w_hi = sb("w_hi", [P, 3, H * DQ], F32R)
        w_lo = sb("w_lo", [P, 3, H * DQ], F32R)
        wo_sb = sb("wo_sb", [P, H * DQ // P, D])
        cwv_sb = sb("cwv_sb", [P, D])
        cwo_sb = sb("cwo_sb", [P, D])
        cwq_sb = sb("cwq_sb", [P, 4, P])
        cwk_hi = sb("cwk_hi", [P, 4, P], F32R)
        cwk_lo = sb("cwk_lo", [P, 4, P], F32R)
        cb = sb("cb", [P, 2, 4])
        cbq_sb = sb("cbq_sb", [P, 4])
        part = sb("part", [P, 4])
        cbrow = sb("cbrow", [P, 2, D])
        router_sb = sb("router_sb", [P, E])
        gu_hi = sb("gu_hi", [P, 2, E * F], F32R)
        gu_lo = sb("gu_lo", [P, 2, E * F], F32R)
        down_sb = sb("down_sb", [P, KB, D])
        ident = sb("ident", [P, P])
        causal = sb("causal", [P, P], BF16)
        minus_half = sb("minus_half", [P, 2])
        x_hi = sb("x_hi", [P, 2 * S], F32R)
        x_lo = sb("x_lo", [P, 2 * S], F32R)
        qkT = sb("qkT", [P, 2, H // 2, 2 * S])
        v_sb = sb("v_sb", [P, H, DQ + 1])
        nmax_s = sb("nmax_s", [P, H])
        masked_s = sb("masked_s", [P, 2, 4, S])
        probs_s = sb("probs_s", [P, 2, 4, S])
        probsT_s = sb("probsT_s", [P, 2, 4, S])
        rsum_s = sb("rsum_s", [P, H])
        cat = sb("cat", [P, NG, 4, DQ])
        catT = sb("catT", [P, 2 * NG, S])
        res1 = sb("res1", [P, D])
        stat1 = sb("stat1", [P, 6])
        mv1 = sb("mv1", [P, 4])
        x1 = sb("x1", [P, D])
        ctx_cur = sb("ctx_cur", [P, 2 * S])
        ctx_hi = sb("ctx_hi", [P, 2 * S], F32R)
        ctx_lo = sb("ctx_lo", [P, 2 * S], F32R)
        mask_cur = sb("mask_cur", [P, S], BF16)
        x1T = sb("x1T", [P, S])
        x1bo = sb("x1bo", [P, D])
        k_f = sb("k_f", [P, 4, 2 * S])
        cwqk_raw = k_f[:].rearrange("p s t -> p (s t)").rearrange("p (a s c) -> p a s c", a=2, s=4)
        k_hi = sb("k_hi", [P, 4, 2 * S], F32R)
        q_f = sb("q_f", [P, 4, S])
        q_hi = sb("q_hi", [P, 4, S], F32R)
        k_stack = sb("k_stack", [P, 4, 2 * S], F32R)
        q_stack = sb("q_stack", [P, 4, S], F32R)
        cv = sb("cv", [P, 2 * HC + WIDE - 1, DC + 1])
        nmax_c = sb("nmax_c", [P, HC])
        masked_c = sb("masked_c", [P, 2, 4, S])
        mask_all = masked_c[:].rearrange("p a h t -> p (a h t)").bitcast(I32).rearrange("p (b t) -> p b t", b=B)
        probs_c = sb("probs_c", [P, 2, 4, S])
        probsT_c = sb("probsT_c", [P, 2, 4, S])
        rsum_c = sb("rsum_c", [P, HC])
        ccat = sb("ccat", [P, HC, DC])
        ccatT = sb("ccatT", [P, S])
        res2 = sb("res2", [P, D])
        stat2 = sb("stat2", [P, 6])
        mv2 = sb("mv2", [P, 4])
        x2_cur = sb("x2_cur", [P, D])
        x2T_cur = sb("x2T_cur", [P, S])
        x2_all = sb("x2_all", [P, B, D])
        x2T_hi = sb("x2T_hi", [P, B * S], F32R)
        x2T_lo = sb("x2T_lo", [P, B * S], F32R)
        logits = sb("logits", [P, B, E])
        r_m = sb("r_m", [P, 4, B])
        r_a = sb("r_a", [P, 6, B, E])
        pos = sb("pos", [P, B, E])
        dense_w = sb("dense_w", [P, B, E])
        NS = 4
        silu = probs_s[:].rearrange("p a h t -> p (a h t)").rearrange("p (a t) -> p a t", a=NS)
        hid = [raw[:].rearrange("p (k t) -> p k t", k=KB), qkT[:].rearrange("p a k t -> p (a k) t")]
        free_s = probsT_s[:].rearrange("p a h t -> p (a h t)")
        acc = free_s[:, 0:2 * TB * D].rearrange("p (c a d) -> p c a d", c=2, a=TB)
        y_out = free_s[:, 2 * TB * D:3 * TB * D].rearrange("p (a d) -> p a d", a=TB)
        keep1, keep2, hot1, hot2, s2 = [
            probs_c[:].rearrange("p a h t -> p (a h t)")[:, i * B * E:(i + 1) * B * E].rearrange("p (b e) -> p b e", b=B)
            for i in range(5)]
        stat3 = sb("stat3", [P, TB, 6])
        mv3 = sb("mv3", [P, TB, 4])

        bank = [ctx.enter_context(nc.psum_tensor(f"bank{i}", [P, 512], F32)) for i in range(8)]
        SA, SB_, SC, TA, TB_, TC, OS, OC = bank
        SCORES = (SA, SB_, SC)
        TURNED = (TA, TB_, TC)

        def q_bank(do_self):
            return SC if do_self else SB_

        def k_banks(first):
            return (OC, OC) if first else (SC, TC)

        Y_BANK = [TA, TB_, OS]

        def gu_bank(i):
            return (TC, SC, OS)[i % 3] if i < NFILL else (SA, SB_, SC, TC)[i % 4]

        (ld_xT, ld_xT_rest, ld_wq, ld_wk, ld_wq_rest, ld_wk_rest, ld_wv, ld_cwqk, ld_x, ld_ctx, ld_mask, ld_wo, ld_cw, ld_gu,
         ld_down) = [
            sem(f"ld_{n}") for n in "xT xT_rest wq wk wq_rest wk_rest wv cwqk x ctx mask wo cw gu down".split()]
        cw_ready = sem("cw_ready")
        stored = sem("stored")
        consts = sem("consts")
        mask_set = sem("mask_set")
        ones_set = sem("ones_set")
        w_hi_done = sem("w_hi_done")
        w_lo_done = sem("w_lo_done")
        gu_split = sem("gu_split")
        (x_split, qk_proj, qk_evac, v_proj, v_evac, rec_s, cat_norm, catT_ps, catT_evac, wo_s, res1_done, stat1_done,
         aggr1_done, var1_done, pow1_done, x1_ready) = [sem(n) for n in (
             "x_split qk_proj qk_evac v_proj v_evac rec_s cat_norm catT_ps catT_evac wo_s res1_done stat1_done "
             "aggr1_done var1_done pow1_done x1_ready").split()]
        scored = {k: sem(f"scored_{k}") for k in "sc"}
        maxed = {k: sem(f"maxed_{k}") for k in "sc"}
        exped = {k: sem(f"exped_{k}") for k in "sc"}
        turned = {k: sem(f"turned_{k}") for k in "sc"}
        turned_evac = {k: sem(f"turned_evac_{k}") for k in "sc"}
        mixed = {k: sem(f"mixed_{k}") for k in "sc"}
        (ctx_ready, ctx_copied, mask_ready, ck_proj, cv_proj, ck_evac, cv_evac, x1T_ps, x1T_evac, cq_proj, cq_evac, k_hi_done,
         q_hi_done, x1bo_done, stack_k, stack_q, rec_c, ccat_norm) = [sem(n) for n in (
             "ctx_ready ctx_copied mask_ready ck_proj cv_proj ck_evac cv_evac x1T_ps x1T_evac cq_proj cq_evac k_hi_done "
             "q_hi_done x1bo_done stack_k stack_q rec_c ccat_norm").split()]
        (ccatT_ps, ccatT_evac, wo_c, res2_done, stat2_done, aggr2_done, var2_done, pow2_done, x2_ready, x2T_ps,
         x2T_evac, logit_ps, logit_evac, x2_split) = [sem(n) for n in (
             "ccatT_ps ccatT_evac wo_c res2_done stat2_done aggr2_done var2_done pow2_done x2_ready x2T_ps "
             "x2T_evac logit_ps logit_evac x2_split").split()]
        (r_step, r_exp_in, r_exp, dense_ready, gated, silued, gate_done, hid_done, down_ps, combined,
         stat3_done, aggr3_done, var3_done, pow3_done, y_ready) = [sem(n) for n in (
             "r_step r_exp_in r_exp dense_ready gated silued gate_done hid_done down_ps combined "
             "stat3_done aggr3_done var3_done pow3_done y_ready").split()]

        def groups(n, do_self):
            return [(k, g, n if k == "s" else n - 1) for k, g in (ORDER if do_self else CROSS_ONLY)]

        def banks(i, do_self):
            return (SCORES[i % 3], TURNED[i % 3]) if do_self else (SCORES[i % 2], TURNED[i % 2])

        def wait(eng, s, value):
            if not isinstance(value, int) or value > 0:
                eng.wait_ge(s, value)

        def wait_apart(eng, *waits):
            waits = [(s, v if isinstance(v, int) else eng.snap(eng.to_reg(v), min_val=0)) for s, v in waits]
            eng.wait_ge(consts, 2)
            for s, v in waits:
                wait(eng, s, v)

        def slots(eng, slot):
            slot(0, 0, True, False, False)
            slot(1, 1, True, True, False)
            with eng.Fori(1, B // 2) as pair:
                slot(pair * 2, 0, True, True, True)
                slot(pair * 2 + 1, 1, True, True, True)
            slot(B, 0, False, True, True)
            slot(B + 1, 1, False, False, True)

        block = ctx.enter_context(nc.Block())

        @block.sync
        def _(sp):
            sp.dma_start(xT_all[:, 0:2 * S], xT[:, 0:2 * S]).then_inc(ld_xT, 16)
            sp.dma_start(w_raw[:, 0, 0:512], wqT[:, 0:512]).then_inc(ld_wq, 16)
            sp.dma_start(w_raw[:, 0, 512:], wqT[:, 512:]).then_inc(ld_wq_rest, 16)
            sp.dma_start(w_raw[:, 2, :], wvT).then_inc(ld_wv, 16)
            sp.dma_start(ctxT_all[:, 0:B * S], ctxT).then_inc(ld_ctx, 16)
            sp.dma_start(cwqk_raw[:, 1], cwkT).then_inc(ld_cwqk, 16)
            sp.dma_start(cwqk_raw[:, 0], cwqT).then_inc(ld_cwqk, 16)
            sp.dma_start(xT_all[:, 2 * S:B * S], xT[:, 2 * S:B * S]).then_inc(ld_xT_rest, 16)
            sp.dma_start(cwv_sb[:], cwvT).then_inc(ld_cw, 16)
            sp.dma_start(cwo_sb[:], cwoT).then_inc(ld_cw, 16)
            sp.dma_start(cb[:, 0], cbq).then_inc(ld_cw, 16)
            sp.dma_start(cb[:, 1], cbk).then_inc(ld_cw, 16)
            sp.dma_start(part[:], parts).then_inc(ld_cw, 16)
            sp.dma_start(cbrow[:, 0, :], cbv.rearrange("(a d) -> a d", a=1).broadcast_to([P, D])).then_inc(ld_cw, 16)
            sp.dma_start(cbrow[:, 1, :], cbo.rearrange("(a d) -> a d", a=1).broadcast_to([P, D])).then_inc(ld_cw, 16)
            sp.dma_start(router_sb[:], routerT).then_inc(ld_cw, 16)
            sp.dma_start(wo_sb[:], woT).then_inc(ld_wo, 16)
            sp.wait_ge(w_lo_done, 5)
            sp.dma_start(gu_raw[:, 0, :], gateT).then_inc(ld_gu, 16)
            sp.dma_start(gu_raw[:, 1, :], upT).then_inc(ld_gu, 16)
            sp.dma_start(down_sb[:], down).then_inc(ld_down, 16)

            for c in range(NCH):
                for tb in range(TB):
                    b = c * TB + tb
                    sp.wait_ge(y_ready, b + 1)
                    sp.dma_start(out[b], y_out[:, tb, :]).then_inc(stored, 16)
            sp.wait_ge(stored, 16 * B)

        @block.gpsimd
        def _(pool):
            def split_x(n):
                wait_apart(pool, (v_proj, 2 * n), (ld_xT if isinstance(n, int) and n == 0 else ld_xT_rest, 16))
                src = xT_all[:, bass.ds(n * S, 2 * S)]
                pool.tensor_copy(x_hi[:], src).then_inc(x_split, 1)
                wait_apart(pool, (x_split, n + 1))
                pool.tensor_tensor(x_lo[:], src, x_hi[:].bitcast(F32), ALU.subtract).then_inc(x_split, 1)

            def split_ctx(n):
                wait_apart(pool, (ck_proj, n), (ld_ctx, 16))
                src = ctxT_all[:, bass.ds(n * S, 2 * S)]
                pool.tensor_copy(ctx_hi[:], src).then_inc(ctx_ready, 1)
                wait_apart(pool, (ctx_ready, n + 1))
                pool.tensor_tensor(ctx_lo[:], src, ctx_hi[:].bitcast(F32), ALU.subtract).then_inc(ctx_ready, 1)

            pool.memset(xT_all[:, B * S:], 0.0)
            pool.memset(ctxT_all[:, B * S:], 0.0)
            pool.memset(ident[:], 0.0)
            pool.memset(causal[:], 0.0)
            pool.memset(minus_half[:], -0.5)
            for e in range(E):
                last = pool.memset(pos[:, :, e:e + 1], float(e - E))
            last.then_inc(consts, 1)
            pool.wait_ge(consts, 1)
            pool.affine_select(out=ident[:], in_=ident[:], compare_op=ALU.not_equal, fill=1.0,
                               base=0, pattern=[[-1, P]], channel_multiplier=1)
            pool.affine_select(out=causal[:], in_=causal[:], compare_op=ALU.is_ge, fill=NEG,
                               base=0, pattern=[[-1, P]], channel_multiplier=1).then_inc(consts, 1)
            split_x(0)
            split_ctx(0)
            pool.wait_ge(ld_cwqk, 32)
            pool.tensor_copy(cwk_hi[:], cwqk_raw[:, 1]).then_inc(cw_ready, 1)
            pool.wait_ge(cw_ready, 1)
            pool.tensor_tensor(cwk_lo[:], cwqk_raw[:, 1], cwk_hi[:].bitcast(F32), ALU.subtract).then_inc(cw_ready, 1)
            pool.tensor_scalar(cwq_sb[:], cwqk_raw[:, 0], DC ** -0.5, None, ALU.mult).then_inc(cw_ready, 1)
            pool.wait_ge(ld_cw, 128)
            pool.tensor_scalar(cbq_sb[:], cb[:, 0], DC ** -0.5, None, ALU.mult).then_inc(cw_ready, 1)
            pool.wait_ge(ld_mask, 16)
            pool.tensor_scalar(mask_add[:], mask_all, 0.0, NEG, ALU.is_equal, ALU.mult).then_inc(mask_set, 1)

            def slot(n, odd, do_self, do_cross, do_post):
                m, l = n - 1, n - 2
                if do_cross:
                    pool.wait_ge(x1_ready, m + 1)
                    wait(pool, res2_done, m)
                    pool.tensor_tensor(x1bo[:], x1[:], cbrow[:, 1, :], ALU.add).then_inc(x1bo_done, 1)
                if do_post:
                    pool.wait_ge(var2_done, l + 1)
                    pool.tensor_tensor(mv2[:, 3:4], mv2[:, 2:3], minus_half[:, 0:1], ALU.pow).then_inc(pow2_done, 1)
                if do_self:
                    pool.wait_ge(ld_gu, 32)
                    raw = gu_raw[:, :, bass.ds(n * WP, WP)]
                    hi, lo = gu_hi[:, :, bass.ds(n * WP, WP)], gu_lo[:, :, bass.ds(n * WP, WP)]
                    pool.tensor_copy(hi, raw).then_inc(gu_split, 1)
                    wait_apart(pool, (gu_split, 2 * n + 1))
                    pool.tensor_tensor(lo, raw, hi.bitcast(F32), ALU.subtract).then_inc(gu_split, 1)
                    if odd:
                        split_x(n + 1)
                        split_ctx(n + 1)
                    else:
                        wait_apart(pool, (cv_proj, n))
                        pool.tensor_copy(ctx_cur[:], ctxT_all[:, bass.ds(n * S, 2 * S)]).then_inc(ctx_copied, 2)
                if do_post:
                    wait_apart(pool, (x2_ready, l + 1))
                    pool.tensor_copy(x2_all[:, bass.ds(l, 1), :].rearrange("p a d -> p (a d)"), x2_cur[:])
                    wait_apart(pool, (x2T_evac, l + 1))
                    hi, lo = x2T_hi[:, bass.ds(l * S, S)], x2T_lo[:, bass.ds(l * S, S)]
                    pool.tensor_copy(hi, x2T_cur[:]).then_inc(x2_split, 1)
                    wait_apart(pool, (x2_split, 2 * l + 1))
                    pool.tensor_tensor(lo, x2T_cur[:], hi.bitcast(F32), ALU.subtract).then_inc(x2_split, 1)
                if do_self:
                    wait_apart(pool, (maxed["c"], NG * n), (mask_set, 1))
                    pool.tensor_copy(mask_cur[:], mask_add[:, bass.ds(n, 1), :].rearrange("p a d -> p (a d)"))\
                        .then_inc(mask_ready, 1)
                    pool.wait_ge(var1_done, n + 1)
                    pool.tensor_tensor(mv1[:, 3:4], mv1[:, 2:3], minus_half[:, 0:1], ALU.pow).then_inc(pow1_done, 1)

            slots(pool, slot)
            for c in range(NCH):
                for tb in range(TB):
                    pool.wait_ge(var3_done, c * TB + tb + 1)
                    pool.tensor_tensor(mv3[:, tb, 3:4], mv3[:, tb, 2:3], minus_half[:, 0:1],
                                       ALU.pow).then_inc(pow3_done, 1)

        @block.scalar
        def _(act):
            act.dma_start(w_raw[:, 1, 0:512], wkT[:, 0:512]).then_inc(ld_wk, 16)
            act.dma_start(w_raw[:, 1, 512:], wkT[:, 512:]).then_inc(ld_wk_rest, 16)
            for (i, cols), ld in zip(W_PARTS, (ld_wq, ld_wk, ld_wq_rest, ld_wk_rest, ld_wv)):
                act.wait_ge(ld, 16)
                act.activation(w_hi[:, i, cols], w_raw[:, i, cols], ACT.Copy, scale=W_SCALE[i]).then_inc(w_hi_done, 1)
            act.dma_start(mask_all, mask.rearrange("b q t -> q b t")).then_inc(ld_mask, 16)
            act.dma_start(x_tok[:], x.rearrange("b q d -> q b d")).then_inc(ld_x, 16)

            def exp(kind, g, n):
                masked, probs, nmax = (masked_s, probs_s, nmax_s) if kind == "s" else (masked_c, probs_c, nmax_c)
                act.wait_ge(maxed[kind], NG * n + g + 1)
                wait(act, turned[kind], NG * n + g - 1)
                for i in range(4):
                    last = act.activation(probs[:, g % 2, i, :], masked[:, g % 2, i, :], ACT.Exp, scale=-1.0,
                                          bias=nmax[:, 4 * g + i:4 * g + i + 1])
                last.then_inc(exped[kind], 1)

            def gate(i):
                act.wait_ge(gated, i + 1)
                wait(act, hid_done, i - NS + 1)
                g = gu_bank(i)[:, 0:CH]
                if i < NFILL:
                    act.activation(silu[:, i % NS, :], g, ACT.Tanh, scale=0.5).then_inc(silued, 1)
                else:
                    act.activation(silu[:, i % NS, :], g, ACT.Silu).then_inc(silued, 1)

            def slot(n, odd, do_self, do_cross, do_post):
                m, l = n - 1, n - 2

                def evac_qk(p):
                    act.wait_ge(qk_proj, 4 * n + p + 1)
                    act.copy(qkT[:, :, p, :], (SA, SB_)[p % 2][:].rearrange("p (a c) -> p a c", a=2)).then_inc(qk_evac, 1)

                def evac_x1T():
                    act.wait_ge(x1T_ps, m + 1)
                    act.copy(x1T[:], TB_[:, 0:S]).then_inc(x1T_evac, 1)

                def round_q():
                    if do_cross:
                        act.wait_ge(cq_evac, m + 1)
                        wait(act, stack_q, m)
                        act.activation(q_hi[:], q_f[:], ACT.Copy, scale=part[:, 0:1]).then_inc(q_hi_done, 1)

                def evac_v(c, b):
                    act.wait_ge(v_proj, 2 * n + c + 1)
                    act.copy(v_sb[:, 8 * c:8 * c + 8, 0:DQ], b[:].rearrange("p (h v) -> p h v", v=DQ)).then_inc(v_evac, 1)

                order = groups(n, do_self)
                live = {"s": do_self, "c": do_cross}

                def at(i):
                    if i < len(order) and live[order[i][0]]:
                        exp(*order[i])

                fill(n, "start", gate)
                first = isinstance(n, int) and n == 0

                def evac_k(a):
                    wait(act, stack_k, n)
                    if first:
                        act.wait_ge(ld_cw, 128)
                        act.wait_ge(cw_ready, 3)
                    act.wait_ge(ck_proj, n + a + 1)
                    for c in range(2):
                        s = 2 * a + c
                        last = act.activation(k_f[:, s, :], k_banks(first)[a][:, c * 2 * S:(c + 1) * 2 * S], ACT.Identity,
                                              bias=cb[:, 1, s:s + 1])
                    last.then_inc(ck_evac, 1)

                def round_k():
                    act.wait_ge(ck_evac, n + 2)
                    act.activation(k_hi[:], k_f[:], ACT.Copy, scale=part[:, 1:2]).then_inc(k_hi_done, 2)

                if do_self and not odd:
                    evac_qk(0)
                    evac_qk(1)
                    if not first:
                        evac_k(0)
                    evac_qk(2)
                    if not first:
                        evac_k(1)
                    evac_qk(3)
                    if do_cross:
                        evac_x1T()
                    for p in range(4, 7):
                        evac_qk(p)
                    round_q()
                    evac_qk(7)
                    at(0)
                elif do_cross and odd:
                    at(0)
                    evac_x1T()
                elif do_cross:
                    fill(n, "ccat", gate)
                    fill(n, "out", gate)
                    evac_x1T()
                    fill(n, "x1", gate)
                    round_q()
                    fill(n, "q", gate)
                    at(0)
                elif do_self and odd:
                    at(0)
                if not do_cross and do_post:
                    fill(n, "ccat", gate)
                    fill(n, "out", gate)
                if do_self:
                    wait(act, mixed["s"], NG * n)
                    if first:
                        act.wait_ge(ones_set, 1)
                    evac_v(0, OS)
                    at(1)
                    if odd:
                        round_q()
                    evac_v(1, TC)
                if do_self and not odd and not first:
                    round_k()

                def evac_turned_c(i):
                    if i in range(len(order)) and order[i][0] == "c" and do_cross:
                        g = order[i][1]
                        act.wait_ge(turned["c"], NG * m + g + 1)
                        wait(act, mixed["c"], NG * m + g - 1)
                        act.copy(probsT_c[:, g % 2].rearrange("p h t -> p (h t)"),
                                 banks(i, do_self)[1][:]).then_inc(turned_evac["c"], 1)

                for i in range(len(order) + 1):
                    if do_self:
                        if i >= 2:
                            at(i)
                        evac_turned_c(i - 1)
                    else:
                        at(i + 1)
                        evac_turned_c(i)
                    if i == (AT_X2 + 1 if do_self else AT_X2_LAST) and do_post:
                        act.wait_ge(x2T_ps, l + 1)
                        act.copy(x2T_cur[:], OC[:, 0:S]).then_inc(x2T_evac, 1)
                    if first and i in AT_K_FIRST:
                        evac_k(AT_K_FIRST.index(i))
                        if i == AT_K_FIRST[1]:
                            round_k()
                    fill(n, i, gate)

            slots(act, slot)

            for i in range(NFILL, 2 * KB):
                gate(i)
                if i == min(NFILL + 11, 2 * KB - 1):
                    act.wait_ge(r_exp_in, 1)
                    act.activation(r_a[:, 4:6].rearrange("p a b e -> p (a b e)"),
                                   r_a[:, 0:2].rearrange("p a b e -> p (a b e)"), ACT.Exp).then_inc(r_exp, 1)
            for i in range(2 * KB, NCH * KB):
                gate(i)

        @block.vector
        def _(dve):
            dve.memset(v_sb[:], 1.0)
            dve.memset(cv[:], 1.0).then_inc(ones_set, 1)
            dve.wait_ge(ones_set, 1)
            for done, (i, cols) in enumerate(W_PARTS):
                dve.wait_ge(w_hi_done, done + 1)
                dve.scalar_tensor_tensor(out=w_lo[:, i, cols], in0=w_raw[:, i, cols], scalar=W_SCALE[i],
                                         in1=w_hi[:, i, cols].bitcast(F32), op0=ALU.mult,
                                         op1=ALU.subtract).then_inc(w_lo_done, 1)

            def group_max(kind, g, n, b):
                masked, nmax, add = (masked_s, nmax_s, causal) if kind == "s" else (masked_c, nmax_c, mask_cur)
                waits = [(scored[kind], NG * n + g + 1), (exped[kind], NG * n + g - 1)]
                if kind == "c" and g == 0:
                    waits.append((mask_ready, n + 1))
                wait_apart(dve, *waits)
                for i in range(4):
                    last = dve.tensor_tensor_reduce(
                        out=masked[:, g % 2, i, :], in0=b[:, i * S:(i + 1) * S], in1=add[:], scale=-1.0,
                        scalar=3e38, op0=ALU.add, op1=ALU.min, accum_out=nmax[:, 4 * g + i:4 * g + i + 1])
                last.then_inc(maxed[kind], 1)

            def evac_turned(kind, g, n, b):
                if kind == "c":
                    return
                dve.wait_ge(turned["s"], NG * n + g + 1)
                wait(dve, mixed["s"], NG * n + g - 1)
                dve.tensor_copy(probsT_s[:, g % 2].rearrange("p h t -> p (h t)"), b[:]).then_inc(turned_evac["s"], 1)

            def normalise_s(g, n):
                o = OS[:, 0:4 * (DQ + 1)].rearrange("p (h v) -> p h v", h=4)
                dve.wait_ge(mixed["s"], NG * n + g + 1)
                r = rsum_s[:, 4 * g:4 * g + 4]
                dve.reciprocal(r, o[:, :, DQ]).then_inc(rec_s, 1)
                dve.wait_ge(rec_s, NG * n + g + 1)
                dve.tensor_tensor(cat[:, g], o[:, :, 0:DQ], spread(r, 2, DQ),
                                  ALU.mult).then_inc(cat_norm, 1)

            def evac_catT(a, n):
                dve.wait_ge(catT_ps, 2 * n + a + 1)
                dve.tensor_copy(catT[:, 4 * a:4 * a + 4, :].rearrange("p c t -> p (c t)"), TC[:]).then_inc(catT_evac, 1)

            def statistics(res, stat, mv, sems, n):
                res_done, stat_done, aggr_done, var_done = sems
                dve.wait_ge(res_done, n + 1)
                dve.bn_stats(stat, res).then_inc(stat_done, 1)
                wait_apart(dve, (stat_done, n + 1))
                dve.bn_aggr(mv[:, 0:2], stat).then_inc(aggr_done, 1)
                dve.wait_ge(aggr_done, n + 1)
                dve.tensor_scalar(mv[:, 2:3], mv[:, 1:2], EPS, None, ALU.add).then_inc(var_done, 1)

            def hidden(i):
                c, k = i // KB, i % KB
                dve.wait_ge(silued, i + 1)
                wait(dve, down_ps, (c - 2) * E + k // FB + 1 if c >= 2 else 0)
                b, t = gu_bank(i), silu[:, i % NS, :]
                if i < NFILL:
                    dve.scalar_tensor_tensor(out=t, in0=t, scalar=1.0, in1=b[:, 0:CH], op0=ALU.add,
                                             op1=ALU.mult).then_inc(gate_done, 1)
                    dve.wait_ge(gate_done, i + 1)
                    dve.scalar_tensor_tensor(out=hid[c % 2][:, k, :], in0=t, scalar=0.5, in1=b[:, CH:2 * CH],
                                             op0=ALU.mult, op1=ALU.mult).then_inc(hid_done, 1)
                else:
                    dve.tensor_tensor(hid[c % 2][:, k, :], t, b[:, CH:2 * CH], ALU.mult).then_inc(hid_done, 1)

            def slot(n, odd, do_self, do_cross, do_post):
                m, l = n - 1, n - 2
                order = groups(n, do_self)
                live = {"s": do_self, "c": do_cross}

                def at(i, f):
                    if 0 <= i < len(order) and live[order[i][0]]:
                        f(*order[i], banks(i, do_self)[f is evac_turned])

                def normalise_x2():
                    dve.wait_ge(pow2_done, l + 1)
                    dve.tensor_scalar(x2_cur[:], res2[:], mv2[:, 0:1], mv2[:, 3:4], ALU.subtract,
                                      ALU.mult).then_inc(x2_ready, 1)

                def stack_of_q():
                    dve.wait_ge(q_hi_done, m + 1)
                    wait(dve, scored["c"], NG * m)
                    dve.scalar_tensor_tensor(out=q_stack[:], in0=q_f[:], scalar=part[:, 2:3], in1=q_hi[:].bitcast(F32),
                                             op0=ALU.mult, op1=ALU.add).then_inc(stack_q, 1)

                fill(n, "start", hidden)
                if odd:
                    at(0, group_max)
                if do_post:
                    dve.wait_ge(ccatT_ps, l + 1)
                    dve.tensor_copy(ccatT[:], TB_[:, 0:S]).then_inc(ccatT_evac, 1)
                    fill(n, "ccat", hidden)
                if odd:
                    at(1, group_max)
                if do_post:
                    dve.wait_ge(wo_c, l + 1)
                    dve.wait_ge(x1bo_done, l + 1)
                    dve.tensor_tensor(res2[:], OC[:, 0:D], x1bo[:], ALU.add).then_inc(res2_done, 1)
                    statistics(res2[:], stat2[:], mv2, (res2_done, stat2_done, aggr2_done, var2_done), l)
                    fill(n, "out", hidden)
                if do_cross:
                    if not do_post:
                        dve.wait_ge(cw_ready, 4)
                    dve.wait_ge(cq_proj, m + 1)
                    dve.tensor_tensor(q_f[:], q_bank(do_self)[:].rearrange("p (s t) -> p s t", s=4), spread(cbq_sb[:], 2, S),
                                      ALU.add).then_inc(cq_evac, 1)
                fill(n, "x1", hidden)
                if do_cross and odd:
                    dve.wait_ge(cv_proj, m + 2)
                    dve.wait_ge(ld_cw, 128)
                    wait(dve, mixed["c"], NG * m)
                    for a in range(2):
                        last = dve.tensor_tensor(cv[:, a * HC:(a + 1) * HC, 0:DC],
                                                 TB_[:, a * D:(a + 1) * D].rearrange("p (h v) -> p h v", v=DC),
                                                 cbrow[:, 0, :].rearrange("p (h v) -> p h v", v=DC), ALU.add)
                    last.then_inc(cv_evac, 2)
                if do_self and not odd:
                    at(0, group_max)
                    at(1, group_max)
                if do_cross:
                    stack_of_q()
                if not do_self:
                    normalise_x2()
                    at(0, group_max)
                    at(1, group_max)
                fill(n, "q", hidden)
                for i in range(len(order) + 1):
                    at(i + 2, group_max)
                    at(i, evac_turned)
                    if i == AT_X2 - 1 and do_post and do_self:
                        normalise_x2()
                    if i >= 1 and order[i - 1][0] == "s" and do_self:
                        normalise_s(order[i - 1][1], n)
                    if i in AT_CAT and do_self:
                        evac_catT(AT_CAT.index(i), n)
                    if i < len(order):
                        fill(n, i, hidden)
                    if i == (AT_LOGITS if do_self else AT_LOGITS_LAST) and do_post:
                        dve.wait_ge(logit_ps, l + 1)
                        dve.tensor_copy(logits[:, bass.ds(l, 1), :].rearrange("p a e -> p (a e)"),
                                        OC[:, 0:E]).then_inc(logit_evac, 1)
                if do_self and not odd:
                    dve.wait_ge(k_hi_done, n + 2)
                    wait(dve, scored["c"], NG * n)
                    dve.scalar_tensor_tensor(out=k_stack[:], in0=k_f[:], scalar=part[:, 3:4], in1=k_hi[:].bitcast(F32),
                                             op0=ALU.mult, op1=ALU.add).then_inc(stack_k, 2)
                if do_self:
                    dve.wait_ge(wo_s, n + 1)
                    dve.wait_ge(ld_x, 16)
                    dve.tensor_tensor(res1[:], OS[:, 0:D], x_tok[:, bass.ds(n, 1), :].rearrange("p a d -> p (a d)"),
                                      ALU.add).then_inc(res1_done, 1)
                    statistics(res1[:], stat1[:], mv1, (res1_done, stat1_done, aggr1_done, var1_done), n)
                if do_cross:
                    o = OC[:, 0:HC * (DC + 1)].rearrange("p (h v) -> p h v", h=HC)
                    dve.wait_ge(mixed["c"], NG * m + NG)
                    dve.reciprocal(rsum_c[:], o[:, :, DC]).then_inc(rec_c, 1)
                    dve.wait_ge(rec_c, m + 1)
                    dve.tensor_tensor(ccat[:], o[:, :, 0:DC], spread(rsum_c[:], 2, DC),
                                      ALU.mult).then_inc(ccat_norm, 1)
                fill(n, len(order), hidden)
                if do_self:
                    dve.wait_ge(pow1_done, n + 1)
                    wait(dve, x1T_ps, n)
                    wait(dve, x1bo_done, n)
                    dve.tensor_scalar(x1[:], res1[:], mv1[:, 0:1], mv1[:, 3:4], ALU.subtract,
                                      ALU.mult).then_inc(x1_ready, 1)

            slots(dve, slot)

            steps = [0]

            def step(ins):
                steps[0] += 1
                ins.then_inc(r_step, 1)
                two, third = (steps[0] - 1) // 3, (steps[0] - 1) % 3
                if third < 2 and NFILL + 2 * two + third < 2 * KB:
                    hidden(NFILL + 2 * two + third)
                dve.wait_ge(r_step, steps[0])

            s = logits[:]
            m1, i1, z1, z2 = (r_m[:, i, :] for i in range(4))
            d1, d2, t, u, e1, e2 = (r_a[:, i] for i in range(6))

            def wide(v):
                return spread(v, 2, E)

            tt = dve.tensor_tensor

            dve.wait_ge(logit_evac, B)

            def one_hot(dst, scores, top):
                step(tt(dst, scores, wide(top), ALU.is_equal))
                step(tt(dst, dst, pos[:], ALU.mult))
                step(dve.tensor_reduce(i1, dst, AX_X, ALU.min))
                step(tt(dst, pos[:], wide(i1), ALU.is_equal))

            def far(dst, diff, top):
                step(dve.scalar_tensor_tensor(out=dst, in0=s, scalar=-1.0, in1=s, op0=ALU.mult, op1=ALU.max))
                step(tt(dst, dst, wide(top), ALU.max))
                step(dve.scalar_tensor_tensor(out=dst, in0=dst, scalar=-JITTER2, in1=diff, op0=ALU.mult,
                                              op1=ALU.is_le))

            step(dve.tensor_reduce(m1, s, AX_X, ALU.max))
            step(tt(d1, s, wide(m1), ALU.subtract))
            one_hot(hot1[:], s, m1)
            far(keep1[:], d1, m1)
            step(dve.scalar_tensor_tensor(out=s2[:], in0=hot1[:], scalar=NEG, in1=s, op0=ALU.mult, op1=ALU.add))
            step(dve.tensor_reduce(z1, s2[:], AX_X, ALU.max))
            step(tt(d2, s, wide(z1), ALU.subtract))
            far(keep2[:], d2, z1)
            step(tt(d2, s2[:], wide(z1), ALU.subtract))
            dve.engine_nop().then_inc(r_exp_in, 1)
            one_hot(hot2[:], s2[:], z1)
            dve.wait_ge(r_exp, 1)
            step(tt(e1, e1, keep1[:], ALU.mult))
            step(tt(e2, e2, keep2[:], ALU.mult))
            step(dve.tensor_reduce(z1, e1, AX_X, ALU.add))
            step(dve.tensor_reduce(z2, e2, AX_X, ALU.add))
            step(dve.reciprocal(z1, z1))
            step(dve.reciprocal(z2, z2))
            step(tt(hot1[:], hot1[:], wide(z1), ALU.mult))
            step(tt(hot2[:], hot2[:], wide(z2), ALU.mult))
            tt(dense_w[:], hot1[:], hot2[:], ALU.add).then_inc(dense_ready, 1)

            def combine(c, e):
                ce = c * E + e
                dve.wait_ge(down_ps, ce + 1)
                if ce == 0:
                    dve.wait_ge(dense_ready, 1)
                for tb in range(TB):
                    b = c * TB + tb
                    if e == 0:
                        wait(dve, y_ready, b - 2 * TB + 1)
                    else:
                        dve.wait_ge(combined, (ce - 1) * TB + tb + 1)
                    dve.scalar_tensor_tensor(out=acc[:, c % 2, tb, :], in0=Y_BANK[ce % 3][:, tb * P:(tb + 1) * P],
                                             scalar=dense_w[:, b, e:e + 1],
                                             in1=x2_all[:, b, :] if e == 0 else acc[:, c % 2, tb, :],
                                             op0=ALU.mult, op1=ALU.add).then_inc(combined, 1)

            def statistics_of_y(c, tb):
                b = c * TB + tb
                dve.wait_ge(combined, (c * E + E - 1) * TB + tb + 1)
                dve.bn_stats(stat3[:, tb, :], acc[:, c % 2, tb, :]).then_inc(stat3_done, 1)
                dve.wait_ge(stat3_done, b + 1)
                dve.bn_aggr(mv3[:, tb, 0:2], stat3[:, tb, :]).then_inc(aggr3_done, 1)
                dve.wait_ge(aggr3_done, b + 1)
                dve.tensor_scalar(mv3[:, tb, 2:3], mv3[:, tb, 1:2], EPS, None, ALU.add).then_inc(var3_done, 1)

            def normalise_y(c, tb):
                b = c * TB + tb
                dve.wait_ge(pow3_done, b + 1)
                wait(dve, stored, 16 * TB * c)
                dve.tensor_scalar(y_out[:, tb, :], acc[:, c % 2, tb, :], mv3[:, tb, 0:1], mv3[:, tb, 3:4],
                                  ALU.subtract, ALU.mult).then_inc(y_ready, 1)

            for c in range(NCH + 1):
                for e in range(E if c < NCH else 3):
                    if c + e:
                        if e == 0:
                            combine(c - 1, E - 1)
                        elif c < NCH:
                            combine(c, e - 1)
                    if c + 2 < NCH:
                        for fb in range(FB):
                            hidden((c + 2) * KB + e * FB + fb)
                    if c and e == 1:
                        for tb in range(TB):
                            statistics_of_y(c - 1, tb)
                    if c and e == 2:
                        for tb in range(TB):
                            normalise_y(c - 1, tb)

        @block.tensor
        def _(pe):
            def split_product(dst, w, xs, start=True):
                (wh, wl), (xh, xl) = w, xs
                pe.matmul(dst, wh, xh, start=start, stop=False)
                pe.matmul(dst, wh, xl, start=False, stop=False)
                return pe.matmul(dst, wl, xh, start=False, stop=True)

            def gate_up(i):
                c, k = i // KB, i % KB
                b = gu_bank(i)
                if i == 2:
                    pe.wait_ge(res1_done, B)
                if k == 0:
                    pe.wait_ge(x2_split, 2 * TB * (c + 1))
                    if c == 0:
                        pe.wait_ge(gu_split, 2 * B)
                wait(pe, hid_done, max([j + 1 for j in range(i) if gu_bank(j) is b], default=0))
                toks = slice(c * CH, (c + 1) * CH)
                cols = slice(k * P, (k + 1) * P)
                for a in range(2):
                    last = split_product(b[:, a * CH:(a + 1) * CH], (gu_hi[:, a, cols], gu_lo[:, a, cols]),
                                         (x2T_hi[:, toks], x2T_lo[:, toks]))
                last.then_inc(gated, 1)

            def keep_warm(times):
                for _ in range(times):
                    pe.matmul(OC[:], x_hi[:, 0:S], w_hi[:, 2, 0:512], start=True, stop=True)

            def score_s(g, n, half, b):
                if not half and g < 2:
                    pe.wait_ge(qk_evac, 4 * n + 7 + g)
                for i, h in enumerate(GROUPS[g]):
                    rows, toks = slice(64 * (h % 2), 64 * (h % 2) + 64), slice(half * S, (half + 1) * S)
                    last = pe.matmul(b[:, i * S:(i + 1) * S], qkT[rows, 0, h // 2, toks], qkT[rows, 1, h // 2, toks],
                                     start=True, stop=True)
                last.then_inc(scored["s"], 1)

            def score_c(j, m, half, b):
                if j == 0:
                    pe.wait_ge(stack_q, m + 1)
                    pe.wait_ge(stack_k, m + 2 - half)
                rows = slice(32 * j, 32 * j + 32)
                for i in range(4):
                    last = pe.matmul(b[:, i * S:(i + 1) * S], q_stack[rows, i, :],
                                     k_stack[rows, i, half * S:(half + 1) * S], start=True, stop=True)
                last.then_inc(scored["c"], 1)

            def turn(kind, g, n, b):
                probs = probs_s if kind == "s" else probs_c
                pe.wait_ge(exped[kind], NG * n + g + 1)
                for i in range(4):
                    last = pe.transpose(b[:, i * S:(i + 1) * S], probs[:, g % 2, i, :], ident[:])
                last.then_inc(turned[kind], 1)

            def mix_s(g, n):
                pe.wait_ge(turned_evac["s"], NG * n + g + 1)
                if g == 0:
                    pe.wait_ge(v_evac, 2 * n + 2)
                else:
                    pe.wait_ge(cat_norm, NG * n + g)
                for i, h in enumerate(GROUPS[g]):
                    last = pe.matmul(OS[:, i * (DQ + 1):(i + 1) * (DQ + 1)], probsT_s[:, g % 2, i, :], v_sb[:, h, :],
                                     start=True, stop=True)
                last.then_inc(mixed["s"], 1)

            def mix_c(j, m, half):
                pe.wait_ge(turned_evac["c"], NG * m + j + 1)
                for i in range(4):
                    h = 4 * j + i
                    last = pe.matmul(OC[:, h * (DC + 1):(h + WIDE) * (DC + 1)], probsT_c[:, j % 2, i, :],
                                     cv[:, half * HC + h:half * HC + h + WIDE, :].rearrange("p h v -> p (h v)"),
                                     start=True, stop=True)
                last.then_inc(mixed["c"], 1)

            def turn_cat(a, n):
                pe.wait_ge(cat_norm, NG * n + 2 * a + 2)
                for i in range(4):
                    g, half = 2 * a + i // 2, i % 2
                    last = pe.transpose(TC[:, i * P:(i + 1) * P],
                                        cat[:, g, 2 * half:2 * half + 2, :].rearrange("p h v -> p (h v)"), ident[:])
                last.then_inc(catT_ps, 1)

            def slot(n, odd, do_self, do_cross, do_post):
                m, l = n - 1, n - 2
                first = isinstance(n, int) and n == 0

                def project_qk(p):
                    b = (SA, SB_)[p % 2]
                    if p == 0:
                        pe.wait_ge(x_split, n + 2)
                        if first:
                            pe.wait_ge(consts, 2)
                    if first and p in (0, 4):
                        pe.wait_ge(w_lo_done, 2 if p == 0 else 4)
                    if p >= 2:
                        pe.wait_ge(qk_evac, 4 * n + p - 1)
                    cols = slice(p * P, (p + 1) * P)
                    for a in range(2):
                        last = split_product(b[:, a * 2 * S:(a + 1) * 2 * S], (w_hi[:, a, cols], w_lo[:, a, cols]),
                                             (x_hi[:], x_lo[:]))
                    last.then_inc(qk_proj, 1)

                def project_v(c):
                    b = (OS, TC)[c]
                    if first:
                        pe.wait_ge(w_lo_done, 5)
                    if c == 0:
                        wait(pe, res1_done, n)
                    elif not odd and not first:
                        pe.wait_ge(ck_evac, n + 2)
                    cols, toks = slice(c * 512, (c + 1) * 512), slice(odd * S, (odd + 1) * S)
                    pe.matmul(b[:], x_hi[:, toks], w_hi[:, 2, cols], start=True, stop=False)
                    pe.matmul(b[:], x_hi[:, toks], w_lo[:, 2, cols], start=False, stop=False)
                    pe.matmul(b[:], x_lo[:, toks], w_hi[:, 2, cols], start=False, stop=True).then_inc(v_proj, 1)

                def turn_ccat():
                    pe.wait_ge(ccat_norm, l + 1)
                    pe.transpose(TB_[:, 0:S], ccat[:].rearrange("p h v -> p (h v)"), ident[:]).then_inc(ccatT_ps, 1)

                def project_out_c():
                    pe.wait_ge(ccatT_evac, l + 1)
                    pe.matmul(OC[:, 0:D], ccatT[:], cwo_sb[:], start=True, stop=True).then_inc(wo_c, 1)

                def turn_x1():
                    pe.wait_ge(x1_ready, m + 1)
                    if do_post:
                        pe.wait_ge(ccatT_evac, l + 1)
                    pe.transpose(TB_[:, 0:S], x1[:], ident[:]).then_inc(x1T_ps, 1)

                def turn_x2():
                    pe.wait_ge(x2_ready, l + 1)
                    pe.transpose(OC[:, 0:S], x2_cur[:], ident[:]).then_inc(x2T_ps, 1)

                def project_kc(a):
                    b = k_banks(first)[a]
                    if first and a:
                        pe.wait_ge(ck_evac, 1)
                    pe.wait_ge(ctx_ready, n + 2)
                    if first:
                        pe.wait_ge(cw_ready, 2)
                    for c in range(2):
                        s = 2 * a + c
                        last = split_product(b[:, c * 2 * S:(c + 1) * 2 * S], (cwk_hi[:, s, :], cwk_lo[:, s, :]),
                                             (ctx_hi[:], ctx_lo[:]))
                    last.then_inc(ck_proj, 1)

                def project_vc():
                    pe.wait_ge(x1T_evac, m + 1)
                    pe.wait_ge(ctx_copied, m + 2)
                    for a in range(2):
                        last = pe.matmul(TB_[:, a * D:(a + 1) * D], ctx_cur[:, a * S:(a + 1) * S], cwv_sb[:], start=True,
                                         stop=True)
                    last.then_inc(cv_proj, 2)

                def project_qc():
                    pe.wait_ge(x1T_evac, m + 1)
                    if do_self and not odd:
                        pe.wait_ge(ck_evac, n + 1)
                    for s in range(4):
                        last = pe.matmul(q_bank(do_self)[:, s * S:(s + 1) * S], cwq_sb[:, s, :], x1T[:], start=True, stop=True)
                    last.then_inc(cq_proj, 1)

                order = groups(n, do_self)
                live = {"s": do_self, "c": do_cross}

                def score(i):
                    if i < len(order):
                        kind, g, row = order[i]
                        if i == (2 if do_self else 1) and do_cross:
                            pe.wait_ge(cq_evac, m + 1)
                        if do_cross and not do_self and i >= 2:
                            pe.wait_ge(maxed["c"], NG * m + i - 1)
                        if live[kind]:
                            (score_s if kind == "s" else score_c)(g, row, odd if kind == "s" else 1 - odd,
                                                                  banks(i, do_self)[0])

                fill(n, "start", gate_up)
                if not odd:
                    if do_self:
                        project_qk(0)
                        project_qk(1)
                        if not first:
                            project_kc(0)
                    if do_post:
                        turn_ccat()
                        fill(n, "ccat", gate_up)
                    if do_self:
                        project_qk(2)
                        if not first:
                            project_kc(1)
                    if do_post:
                        project_out_c()
                        fill(n, "out", gate_up)
                    if do_self:
                        project_qk(3)
                    if do_cross:
                        turn_x1()
                        fill(n, "x1", gate_up)
                    if do_self:
                        project_qk(4)
                    if do_cross:
                        project_qc()
                        fill(n, "q", gate_up)
                    if do_self:
                        project_qk(5)
                        project_qk(6)
                        project_qk(7)
                    score(0)
                    score(1)
                    if do_self:
                        project_v(0)
                        project_v(1)
                else:
                    score(0)
                    score(1)
                    if do_post:
                        turn_ccat()
                        fill(n, "ccat", gate_up)
                    if do_self:
                        project_v(0)
                    if do_post:
                        project_out_c()
                        fill(n, "out", gate_up)
                    if do_cross:
                        turn_x1()
                    if do_self:
                        project_v(1)
                    if do_cross:
                        project_qc()
                        project_vc()
                for i in range(len(order) + 1):
                    score(i + 2)
                    if first and i in AT_K_FIRST:
                        project_kc(AT_K_FIRST.index(i))
                    if first and i > AT_K_FIRST[1]:
                        pe.wait_ge(ck_evac, 2)
                        keep_warm(4)
                    if i < len(order) and live[order[i][0]]:
                        if i == 1 and do_cross:
                            pe.wait_ge(x1T_evac, m + 1)
                            if odd:
                                pe.wait_ge(cv_evac, m + 2)
                        if i == 2 and do_self:
                            pe.wait_ge(v_evac, 2 * n + 2)
                        if i == 5 and do_self:
                            pe.wait_ge(catT_evac, 2 * n + 1)
                        turn(*order[i], banks(i, do_self)[1])
                    if i >= 1 and live[order[i - 1][0]]:
                        kind, g, row = order[i - 1]
                        if (kind, g) == ("c", 0) and do_post:
                            pe.wait_ge(logit_evac, l + 1)
                        if kind == "s":
                            mix_s(g, row)
                        else:
                            mix_c(g, row, 1 - odd)
                    if i in AT_CAT and do_self:
                        turn_cat(AT_CAT.index(i), n)
                    if i == (AT_X2 if do_self else AT_X2_LAST) and do_post:
                        turn_x2()
                    fill(n, i, gate_up)
                    if i == (AT_LOGITS if do_self else AT_LOGITS_LAST) and do_post:
                        pe.wait_ge(x2T_evac, l + 1)
                        pe.matmul(OC[:, 0:E], x2T_cur[:], router_sb[:], start=True, stop=True).then_inc(logit_ps, 1)
                    if i == AT_OUT and do_self:
                        pe.wait_ge(catT_evac, 2 * n + 2)
                        if first:
                            pe.wait_ge(ld_wo, 16)
                        for k in range(2 * NG):
                            last = pe.matmul(OS[:, 0:D], catT[:, k, :], wo_sb[:, k, :], start=(k == 0),
                                             stop=(k == 2 * NG - 1))
                        last.then_inc(wo_s, 1)

            slots(pe, slot)

            def down_product(c, e):
                ce = c * E + e
                pe.wait_ge(hid_done, (ce + 1) * FB)
                wait(pe, combined, TB * (ce - 2))
                for tb in range(TB):
                    for fb in range(FB):
                        last = pe.matmul(Y_BANK[ce % 3][:, tb * P:(tb + 1) * P],
                                         hid[c % 2][:, e * FB + fb, tb * P:(tb + 1) * P], down_sb[:, e * FB + fb, :],
                                         start=(fb == 0), stop=(fb == FB - 1))
                last.then_inc(down_ps, 1)

            for i in range(NFILL, 2 * KB):
                gate_up(i)
            pe.wait_ge(ld_down, 16)
            for c in range(NCH):
                for e in range(E):
                    down_product(c, e)
                    if c + 2 < NCH:
                        for fb in range(FB):
                            gate_up((c + 2) * KB + e * FB + fb)


def kernel(**inputs):
    import numpy as np
    import concourse.bacc as bacc
    from concourse.bass_utils import run_bass_kernel_spmd

    a = {k: np.asarray(v) for k, v in inputs.items()}
    B, S, D = a["x"].shape
    w_o = a["L0_attn_w_o"]
    H, DQ, _ = a["L0_attn_w_q"].shape
    E, F, _ = a["L0_ffn_w_gate"].shape
    order = [h for group in head_order(H) for h in group]
    wo_rows = w_o.T.reshape(H, DQ, D)[order].reshape(H * DQ // P, P, D)
    down = a["L0_ffn_w_down"].transpose(0, 2, 1).reshape(E * F // P, P, D)
    row = np.arange(P)
    stack = 8 * (4 * (row // 32) + np.arange(4)[:, None]) + row % 8
    r = row % 32 // 8
    lower = np.stack([r % 2, r // 2], axis=1).astype(np.float32)
    laid = {
        "x": a["x"],
        "xT": a["x"].transpose(2, 0, 1).reshape(D, B * S),
        "ctxT": a["ctx_1024"].transpose(2, 0, 1).reshape(D, B * S),
        "mask": a["mask_BxSxS2_ik1"],
        "wqT": a["L0_attn_w_q"].reshape(H * DQ, D).T,
        "wkT": a["L0_attn_w_k"].reshape(H * DQ, D).T,
        "wvT": a["L0_attn_w_v"].reshape(H * DQ, D).T,
        "woT": wo_rows.transpose(1, 0, 2),
        "cwqT": a["L0_xattn_Wq"][stack].transpose(2, 0, 1),
        "cwkT": a["L0_xattn_Wk"][stack].transpose(2, 0, 1),
        "cwvT": a["L0_xattn_Wv"].T,
        "cwoT": a["L0_xattn_Wo"].T,
        "cbq": a["L0_xattn_bq"][stack].T,
        "cbk": a["L0_xattn_bk"][stack].T,
        "cbv": a["L0_xattn_bv"],
        "cbo": a["L0_xattn_bo"],
        "parts": np.concatenate([1 - 2 * lower, lower], axis=1),
        "routerT": a["L0_ffn_router_w"].T,
        "gateT": a["L0_ffn_w_gate"].reshape(E * F, D).T,
        "upT": a["L0_ffn_w_up"].reshape(E * F, D).T,
        "down": down.transpose(1, 0, 2),
    }
    laid = {k: np.ascontiguousarray(v) for k, v in laid.items()}
    nc = bacc.Bacc("TRN2", target_bir_lowering=False, num_devices=1)
    args = [nc.dram_tensor(f"in_{k}", v.shape, mybir.dt.from_np(v.dtype), kind="ExternalInput").ap()
            for k, v in laid.items()]
    out = nc.dram_tensor("out_0", (B, S, D), F32, kind="ExternalOutput").ap()
    build_decoder(nc, *args, out)
    r = run_bass_kernel_spmd(nc, [{f"in_{k}": v for k, v in laid.items()}], core_ids=[0])
    return r.results[0]["out_0"]
```
